# Optimizing a Trainium2 kernel written in Bass

```python
import numpy as np
import jax
import jax.numpy as jnp

def _softmax(x, axis=-1):
    return jax.nn.softmax(x, axis=axis)

def _gelu(x):
    return jax.nn.gelu(x, approximate=True)

def _silu(x):
    return jax.nn.silu(x)

def _sigmoid(x):
    return jax.nn.sigmoid(x)

def _layernorm(x, axis=-1, eps=1e-05):
    m = jnp.mean(x, axis=axis, keepdims=True)
    v = jnp.var(x, axis=axis, keepdims=True)
    return (x - m) / jnp.sqrt(v + eps)

def _scatter_add(tgt, idx, src, axis=0):
    return tgt.at[idx].add(src)

def _segment_sum(src, seg, n):
    return jax.ops.segment_sum(src, seg, n)
kernel_name = 'mk_flamingo_gated_d1_seqx_r8_ac2102'

def setup_inputs(seed: int=0):
    np.random.seed(seed)
    _w = jnp.asarray

    def _rec_inputs():
        import jax
        import jax.numpy as jnp
        _rk = jax.random.key(seed)
        x = 7.22e-05 + 1 * jax.random.normal(jax.random.fold_in(_rk, 1), (16, 256, 128), jnp.float32)
        _lenS = 256 - jax.random.randint(jax.random.fold_in(_rk, 7), (16,), 0, max(1, 256 // 4) + 1, jnp.int32)
        _lenS2 = 1601 - jax.random.randint(jax.random.fold_in(_rk, 8), (16,), 0, max(1, 1601 // 4) + 1, jnp.int32)
        _ctx_1024P = jax.random.normal(jax.random.fold_in(_rk, 11), (16, 16, 128), jnp.float32)
        _ctx_1024c = jax.random.dirichlet(jax.random.fold_in(_rk, 511), 0.3 * jnp.ones((16,), jnp.float32), (16, 1601))
        _ctx_1024t = jnp.einsum('bsk,bkd->bsd', _ctx_1024c, _ctx_1024P)
        _ctx_1024t = _ctx_1024t * jax.lax.rsqrt(jnp.mean(jnp.square(_ctx_1024t)) + 1e-12) * 0.953939
        ctx_1024 = 4.13588e-05 + 0.999923 * (_ctx_1024t + 0.3 * jax.random.normal(jax.random.fold_in(_rk, 611), (16, 1601, 128), jnp.float32))
        _validS = jnp.arange(256)[None, :] < _lenS[:, None]
        _validS2 = jnp.arange(1601)[None, :] < _lenS2[:, None]
        _causal = jnp.tril(jnp.ones((256, 256), dtype=bool))
        mask_BxS2_if1 = jnp.where(jnp.ones((16, 1601), dtype=bool), 1, 0).astype(jnp.int32)
        _g = jax.random.normal(jax.random.fold_in(_rk, 9001), (2, 1), jnp.float32)
        _g = jnp.sign(_g) * jnp.maximum(jnp.abs(_g), 1.0) + (_g == 0) * 1.0
        g_xattn = _g[0]
        g_ffn = _g[1]
        return (x, ctx_1024, mask_BxS2_if1, g_xattn, g_ffn)
    x, ctx_1024, mask_BxS2_if1, g_xattn, g_ffn = _rec_inputs()

    def _L0_xattn_setup():
        import jax, jax.numpy as jnp
        import numpy as np
        D_MODEL = 128
        N_HEADS = 16
        D_HEAD = D_MODEL // N_HEADS
        NEG_INF = jnp.float32(-1e+30)
        key = jax.random.key(seed)
        kq, kk, kv, kwq, kwk, kwv, kwo = jax.random.split(key, 7)
        B, L = (4, 256)
        s = 1.0 / np.sqrt(D_MODEL)
        return {'query': jax.random.normal(kq, (B, L, D_MODEL), jnp.float32), 'key': jax.random.normal(kk, (B, L, D_MODEL), jnp.float32), 'value': jax.random.normal(kv, (B, L, D_MODEL), jnp.float32), 'attention_mask': jnp.ones((B, L), jnp.int32), 'Wq': jax.random.normal(kwq, (D_MODEL, D_MODEL), jnp.float32) * s, 'Wk': jax.random.normal(kwk, (D_MODEL, D_MODEL), jnp.float32) * s, 'Wv': jax.random.normal(kwv, (D_MODEL, D_MODEL), jnp.float32) * s, 'Wo': jax.random.normal(kwo, (D_MODEL, D_MODEL), jnp.float32) * s}
    _L0_xattn_all = _L0_xattn_setup()
    _L0_xattn_in = {k: v for k, v in _L0_xattn_all.items() if k in ('Wq', 'Wk', 'Wv', 'Wo')}
    del _L0_xattn_all

    def _L0_ffn_setup():
        import jax, jax.numpy as jnp
        import numpy as np
        key = jax.random.key(seed)
        ks = jax.random.split(key, 5)
        B, T, D, E = (4, 256, 128, 8)
        inputs = jax.random.normal(ks[0], (B, T, D), dtype=jnp.float32)
        Wr = jax.random.normal(ks[1], (D, E), dtype=jnp.float32) * 0.02
        br = jnp.zeros((E,), dtype=jnp.float32)
        W1 = jax.random.normal(ks[2], (E, D, D), dtype=jnp.float32) * 0.02
        b1 = jnp.zeros((E, D), dtype=jnp.float32)
        W2 = jax.random.normal(ks[3], (E, D, D), dtype=jnp.float32) * 0.02
        b2 = jnp.zeros((E, D), dtype=jnp.float32)
        return {'inputs': inputs, 'Wr': Wr, 'br': br, 'W1': W1, 'b1': b1, 'W2': W2, 'b2': b2}
    _L0_ffn_all = _L0_ffn_setup()
    _L0_ffn_in = {k: v for k, v in _L0_ffn_all.items() if k in ('Wr', 'br', 'W1', 'b1', 'W2', 'b2')}
    del _L0_ffn_all
    return {'x': x, 'ctx_1024': ctx_1024, 'mask_BxS2_if1': mask_BxS2_if1, 'g_xattn': g_xattn, 'g_ffn': g_ffn, 'L0_xattn_Wq': _L0_xattn_in['Wq'], 'L0_xattn_Wk': _L0_xattn_in['Wk'], 'L0_xattn_Wv': _L0_xattn_in['Wv'], 'L0_xattn_Wo': _L0_xattn_in['Wo'], 'L0_ffn_Wr': _L0_ffn_in['Wr'], 'L0_ffn_br': _L0_ffn_in['br'], 'L0_ffn_W1': _L0_ffn_in['W1'], 'L0_ffn_b1': _L0_ffn_in['b1'], 'L0_ffn_W2': _L0_ffn_in['W2'], 'L0_ffn_b2': _L0_ffn_in['b2']}

def reference(x, ctx_1024, mask_BxS2_if1, g_xattn, g_ffn, L0_xattn_Wq, L0_xattn_Wk, L0_xattn_Wv, L0_xattn_Wo, L0_ffn_Wr, L0_ffn_br, L0_ffn_W1, L0_ffn_b1, L0_ffn_W2, L0_ffn_b2):
    import jax
    import jax.numpy as jnp

    def _L0_xattn_ref(query, key, value, attention_mask, Wq, Wk, Wv, Wo):
        import jax, jax.numpy as jnp
        import numpy as np
        D_MODEL = 128
        N_HEADS = 16
        D_HEAD = D_MODEL // N_HEADS
        NEG_INF = jnp.float32(-1e+30)
        B, Lq, D = query.shape
        Lk = key.shape[1]

        def split_heads(x, W, L):
            return (x @ W.T).reshape(B, L, N_HEADS, D_HEAD).transpose(0, 2, 1, 3)
        q = split_heads(query, Wq, Lq)
        k = split_heads(key, Wk, Lk)
        v = split_heads(value, Wv, Lk)
        scores = jnp.einsum('bhqd,bhkd->bhqk', q, k) / jnp.sqrt(jnp.float32(D_HEAD))
        causal = jnp.triu(jnp.ones((Lq, Lk), bool), k=1)
        scores = jnp.where(causal[None, None], NEG_INF, scores)
        key_valid = attention_mask.astype(bool)[:, None, None, :]
        scores = jnp.where(key_valid, scores, NEG_INF)
        attn = jax.nn.softmax(scores, axis=-1)
        ctx = jnp.einsum('bhqk,bhkd->bhqd', attn, v)
        ctx = ctx.transpose(0, 2, 1, 3).reshape(B, Lq, D)
        return ctx @ Wo.T

    def _L0_ffn_ref(inputs, Wr, br, W1, b1, W2, b2):
        import jax, jax.numpy as jnp
        import numpy as np
        B, T, D = inputs.shape
        E = Wr.shape[1]
        x = inputs.reshape(B * T, D)
        N = x.shape[0]
        C = N // E
        logits = x @ Wr + br
        probs = jax.nn.softmax(logits, axis=-1)
        gate = jnp.max(probs, axis=-1, keepdims=True)
        idx = jnp.argmax(probs, axis=-1)
        mask = jax.nn.one_hot(idx, E, dtype=jnp.float32)
        pos = (jnp.cumsum(mask, axis=0) * mask).astype(jnp.int32)
        mask = mask * (pos < C).astype(jnp.float32)
        mask_flat = jnp.sum(mask, axis=-1, keepdims=True)
        gate = gate * mask_flat
        combine = (gate * mask_flat * jax.nn.one_hot(idx, E, dtype=jnp.float32))[..., None] * jax.nn.one_hot(pos, C, dtype=jnp.float32)
        dispatch = combine
        expert_in = jnp.einsum('nd,nec->ecd', x, dispatch)
        h = jax.nn.relu(jnp.einsum('ecd,edf->ecf', expert_in, W1) + b1[:, None, :])
        eo = jnp.einsum('ecf,efd->ecd', h, W2) + b2[:, None, :]
        out = jnp.einsum('ecd,nec->nd', eo, combine)
        return out.reshape(B, T, D)
    x = x + jnp.tanh(g_xattn[0]) * _L0_xattn_ref(_layernorm(x, axis=-1), ctx_1024, ctx_1024, mask_BxS2_if1, L0_xattn_Wq, L0_xattn_Wk, L0_xattn_Wv, L0_xattn_Wo)
    x = x + jnp.tanh(g_ffn[0]) * _L0_ffn_ref(_layernorm(x, axis=-1), L0_ffn_Wr, L0_ffn_br, L0_ffn_W1, L0_ffn_b1, L0_ffn_W2, L0_ffn_b2)
    return x

_drawn_inputs = setup_inputs


def setup_inputs(seed=0):
    import zlib

    import numpy as np

    out = dict(_drawn_inputs(seed))
    spreads = {'L0_ffn_br': (0.0, 0.61), 'L0_ffn_b1': (0.0, 0.8), 'L0_ffn_b2': (0.0, 0.688)}
    factors = {'L0_ffn_Wr': 5.074, 'L0_ffn_W1': 8.0, 'L0_ffn_W2': 8.0}
    for name, (base, spread) in spreads.items():
        noise = np.random.default_rng([zlib.crc32(name.encode()), seed]).standard_normal(out[name].shape)
        drawn = base * np.exp(spread * noise) if base else spread * noise
        out[name] = jnp.asarray(drawn.astype(out[name].dtype))
    for name, factor in factors.items():
        out[name] = (out[name] * factor).astype(out[name].dtype)
    return out
```

```python
from contextlib import ExitStack

import concourse.bass as bass
from concourse import mybir

ALU = mybir.AluOpType
ACT = mybir.ActivationFunctionType
AX_X = mybir.AxisListType.X
F32 = mybir.dt.float32
BF16 = mybir.dt.bfloat16
I32 = mybir.dt.int32

P = 128
NEG = -1e30
MAX_FLOOR = -1e29
DEAD_AT = 5e28
FAR = 1.0e6
EPS = 1e-5


class Batch:

    def __init__(self, i, k):
        self.i, self.k = i, k
        self.par = k % 2

    def num(self):
        return self.i * 2 + self.k

    def minus(self, n):
        return Batch(self.i, self.k - n)

    def count(self, per, done):
        return self.i * (2 * per) + (self.k * per + done)

    def landed(self, dmas):
        return self.i * (16 * dmas) + (self.k // 2 + 1) * 16 * dmas


def wait(eng, sem, value):
    if not (isinstance(value, int) and value <= 0):
        eng.wait_ge(sem, value)


def wait_apart(eng, sem, value, passed):
    if isinstance(value, int):
        wait(eng, sem, value)
    else:
        eng.wait_ge(sem, value).then_inc(passed, 1)


class Steps:

    def __init__(self, eng, sem, batch, per, start=0):
        self.eng, self.sem, self.batch, self.per, self.n = eng, sem, batch, per, start

    def did(self, ins):
        ins.then_inc(self.sem, 1)
        self.n += 1
        assert self.n <= self.per

    def settle(self):
        self.eng.wait_ge(self.sem, self.batch.count(self.per, self.n))


def build(nc, x, ctx, ctx_t, mask, g_xattn, g_ffn, wq_t, wk_t, wv_t, wo_t, wr, br, w1, b1, w2, b2, out):
    B, L, D = x.shape
    LK = ctx.shape[1]
    E = wr.shape[1]
    H = 16
    DH = D // H
    N = B * L
    C = N // E
    NQ = L // P
    QUADS = H // 4
    LOADS = 3 * QUADS
    SCALE = float(DH) ** -0.5
    PARTS = 6
    KROWS = DH * PARTS
    SROWS = KROWS + 1
    TROWS = KROWS + 4
    VW = 32
    HW = 16
    RW = 2 * D + 2
    CC = C // P
    FULL = LK // P
    REST = LK - FULL * P
    assert D == P and L == 2 * P and N % E == 0

    x_t = x.rearrange("b (j p) d -> b p j d", p=P)
    out_t = out.rearrange("b (j p) d -> b p j d", p=P)
    out_rows = out.rearrange("b l d -> (b l) d")
    qk_dram = nc.dram_tensor("qk_parts", [2, P, PARTS, 2 * L], BF16, kind="Internal").ap()
    kb_dram = nc.dram_tensor("key_bias", [B, L], BF16, kind="Internal").ap()
    vm_dram = nc.dram_tensor("value_mean", [B, D], F32, kind="Internal").ap()
    rows_dram = nc.dram_tensor("expert_rows", [N, RW], F32, kind="Internal").ap()

    with ExitStack() as stack:
        def sb(name, shape, dt=F32):
            return stack.enter_context(nc.sbuf_tensor(name, shape, dt))

        def ps(name, shape, dt=F32):
            return stack.enter_context(nc.psum_tensor(name, shape, dt))

        def sem(name):
            return stack.enter_context(nc.semaphore(name))

        def sems(name, n=2):
            return [sem(f"{name}{i}") for i in range(n)]

        ident = sb("ident", [P, P])
        ident_b = sb("ident_b", [P, P], BF16)
        causal = sb("causal", [P, P], BF16)
        tri = sb("tri", [P, P], BF16)
        ones_b = sb("ones_b", [P, P], BF16)
        wq_s, wk_s, wv_s, wo_s = (sb(n, [P, D]) for n in ("wq_s", "wk_s", "wv_s", "wo_s"))
        wr_s = sb("wr_s", [P, E])
        br_s = sb("br_s", [P, E])
        gates = sb("gates", [P, 2])
        tg = sb("tg", [P, 2])
        rank = sb("rank", [P, 1, E])
        slot0 = sb("slot0", [P, 1, E])
        mean_w = sb("mean_w", [P, 1])
        filler = sb("filler", [P, RW])
        mask_s = sb("mask_s", [B, L], I32)
        kb_s = sb("kb_s", [B, L], BF16)
        mask0 = sb("mask0", [1, B], I32)
        no_key = sb("no_key", [1, B])
        any_dead = sb("any_dead", [1, 1], I32)
        ctx_sum = sb("ctx_sum", [P, B, D])
        ctx_all = sb("ctx_all", [P, FULL + 1, D])
        csum_t = sb("csum_t", [P, B])
        vmean = sb("vmean", [B, D])
        mark = sb("mark", [1, 1])

        x_in = sb("x_in", [P, 2, NQ, D])
        ctx_in = sb("ctx_in", [P, 2, L])
        x_res = sb("x_res", [P, 2, NQ, D])
        vm_in = sb("vm_in", [P, 2, D])
        lna_st = sb("lna_st", [P, NQ, 6])
        lna_mv = sb("lna_mv", [P, NQ, 2])
        lna_ve = sb("lna_ve", [P, NQ])
        lna_rs = sb("lna_rs", [P, NQ])
        half = sb("half", [P, NQ])
        xn = sb("xn", [P, 2, NQ, D])
        xn_t = sb("xn_t", [P, L])
        parts = sb("parts", [P, 2, 3, 2 * L], BF16)
        resid = sb("resid", [P, 2 * L])
        qk = [sb(f"qk{i}", [64, H, 2 * L], BF16) for i in range(2)]
        v_aug = sb("v_aug", [P, 2, NQ, H, VW])
        max_far = sb("max_far", [P, H, 2])
        max_near = sb("max_near", [P, H])
        max_tmp = sb("max_tmp", [P, 8])
        neg_max = sb("neg_max", [P, NQ, 8])
        neg_res = sb("neg_res", [P, NQ, 8])
        m3 = sb("m3", [P, 2, NQ, 3, 8], BF16)
        m3_t = sb("m3_t", [24, 2, L], BF16)
        dead = sb("dead", [P, 2, NQ, 1])
        pt = sb("pt", [P, 2, 4 * (L + P)])
        o_sb = sb("o_sb", [P, 2 * L])
        l_sum = sb("l_sum", [P, NQ, H])
        l_inv = sb("l_inv", [P, NQ, H])
        cx_n = sb("cx_n", [P, NQ, H, DH])
        cx_f = sb("cx_f", [P, NQ, D])
        cx_t = sb("cx_t", [P, L])
        rows = sb("rows", [P, 2, NQ, RW])
        lnb_st = sb("lnb_st", [P, NQ, 6])
        lnb_mv = sb("lnb_mv", [P, NQ, 2])
        lnb_ve = sb("lnb_ve", [P, NQ])
        lnb_rs = sb("lnb_rs", [P, NQ])
        x2n = sb("x2n", [P, NQ, D])
        x2n_t = sb("x2n_t", [P, L])
        lg = sb("lg", [P, NQ, E])
        lg_max = sb("lg_max", [P, NQ])
        lg_d = sb("lg_d", [P, NQ, E])
        lg_e = sb("lg_e", [P, NQ, E])
        e_sum = sb("e_sum", [P, NQ])
        gate = sb("gate", [P, NQ])
        w_rank = sb("w_rank", [P, NQ, E])
        w_best = sb("w_best", [P, NQ])
        onehot = sb("onehot", [P, NQ, E], BF16)
        carry = sb("carry", [P, 1, E])
        pos = sb("pos", [P, NQ, E])
        picked = sb("picked", [P, 2 * NQ, E])
        pick_sum = sb("pick_sum", [P, 2 * NQ])
        over = sb("over", [P, NQ])
        slot = sb("slot", [P, NQ])
        slot_i = sb("slot_i", [P, 2, NQ], I32)
        token = sb("token", [P, NQ])

        w1_s = sb("w1_s", [P, 2, D])
        w2_s = sb("w2_s", [P, 2, D])
        b1_s = sb("b1_s", [P, 2, 1])
        b2_s = sb("b2_s", [P, 2, D])
        er = sb("er", [P, 2, CC, RW])
        e_in_t = sb("e_in_t", [P, C])
        e_h = sb("e_h", [P, C])
        e_tmp = sb("e_tmp", [P, CC, D])
        e_out = sb("e_out", [P, 2, CC, D])
        e_tok = sb("e_tok", [P, 2, CC], I32)

        s_ps = [ps(f"s_ps{i}", [P, 512]) for i in range(2)]
        t_ps = [ps(f"t_ps{i}", [P, 512]) for i in range(3)]
        o_ps = ps("o_ps", [P, 512])
        ma = ps("ma", [P, 512])
        mb = ps("mb", [P, 512])
        ma_b = ma[:, :].bitcast(BF16)
        mb_b = mb[:, :].bitcast(BF16)

        w_in = sem("weights_in")
        g_in = sem("gates_in")
        mask_in = sem("mask_in")
        mask0_in = sem("mask0_in")
        kb_ready = sem("key_bias_ready")
        kb_out = sem("key_bias_out")
        fill_out = sem("filler_out")
        const_base = sem("const_base")
        const_ready = sem("const_ready")
        vconst = sem("vector_consts")
        tg_ready = sem("tanh_ready")
        dead_found = sem("dead_found")
        all_in = sem("all_ctx_in")
        all_add = sem("all_ctx_added")
        csum_ready = sem("ctx_sum_ready")
        csum_ps = sem("ctx_sum_turned")
        csum_sb = sem("ctx_sum_copied")
        vmean_ps = sem("value_mean_made")
        vmean_sb = sem("value_mean_copied")
        vmean_out = sem("value_mean_out")

        sp_passed = sem("sp_passed")
        pool_passed = sem("pool_passed")
        dve_passed = sem("vector_passed")

        x_got = sems("x_got")
        ctx_got = sems("ctx_got")
        res_got = sems("residual_got")
        lna = sem("lna_steps")
        lna_pow = sem("lna_pow")
        xt_ps = sem("xt_turned")
        xt_sb = sem("xt_copied")
        qk_ps = sem("qk_made")
        qk_hi = sem("qk_hi")
        qk_res = sem("qk_res")
        qk_mid = sem("qk_mid")
        qk_lo = sem("qk_lo")
        parts_out = sems("parts_out")
        stack_in = [sems(f"stack_in{i}_") for i in range(2)]
        v_ps = sem("v_made")
        v_sb = sem("v_copied")
        s_made = sem("s_made")
        s_max = sem("s_max")
        mch = sem("max_steps")
        m_ps = sem("m_turned")
        m_sb = sem("m_copied")
        m_in = [sems(f"m_in{i}_") for i in range(2)]
        t_made = sem("t_made")
        t_exp = sem("t_exp")
        t_masked = sem("t_masked")
        pv = sem("pv_made")
        o_copied = sem("o_copied")
        o_turned = sem("o_turned")
        cxn = sem("cx_steps")
        cxf = sem("cx_fixed")
        cx_ps = sem("cx_turned")
        cx_sb = sem("cx_copied")
        at_ps = sem("attn_made")
        x2_ready = sem("x2_ready")
        x2_out = sems("x2_out")
        lnb = sem("lnb_steps")
        lnb_pow = sem("lnb_pow")
        x2t_ps = sem("x2t_turned")
        x2t_sb = sem("x2t_copied")
        lg_ps = sem("logits_made")
        rt = sem("route_steps")
        e_ready = sem("exp_ready")
        cum_ps = sem("counts_made")
        rs = sem("row_steps")
        sent = sems("rows_sent")

        ew_in = sems("expert_weights_in")
        er_in = sems("expert_rows_in")
        ei_ps = sem("expert_in_turned")
        ei_sb = sem("expert_in_copied")
        eh_ps = sem("expert_h_made")
        eh_sb = sem("expert_h_copied")
        eo_ps = sem("expert_out_made")
        eo = sem("expert_out_steps")
        eo_out = sems("expert_out_sent")

        def heads(quad):
            first = (quad // 2) * 8 + quad % 2
            return [first + 2 * g for g in range(4)]

        FIRST, LAST = 3, 13
        assert (LAST - FIRST) % 2 == 0

        def ticks(eng, tick, between=None):
            def run(i, k):
                t = Batch(i, k)
                known = isinstance(i, int)
                on = [not known or 0 <= k - n < B for n in (-2, -1, 0, 1, 2)]
                tick(t.minus(-2), t.minus(-1), t, t.minus(1), t.minus(2), on)
            for k in range(-2, FIRST):
                run(0, k)
                if between and k == 0:
                    between()
            with eng.Fori(0, (LAST - FIRST) // 2) as i:
                for k in range(2):
                    run(i, FIRST + k)
            for k in range(LAST, B + 2):
                run(0, k)

        def experts(eng, expert):
            for k in range(2):
                expert(Batch(0, k))
            with eng.Fori(0, (E - 2) // 2) as i:
                for k in range(2):
                    expert(Batch(i, 2 + k))

        block = stack.enter_context(nc.Block())

        @block.sync
        def _(sp):
            with nc.allow_non_contiguous_dma(reason="one mask entry of each batch"):
                sp.dma_start(mask0[:, :], mask[:, 0:1].rearrange("b o -> o b")).then_inc(mask0_in, 16)
            sp.dma_start(mask_s[:, :], mask[:, 0:L]).then_inc(mask_in, 16)
            sp.dma_start(gates[:, 0:1], g_xattn.unsqueeze(0).partition_broadcast(P)).then_inc(g_in, 16)
            sp.dma_start(gates[:, 1:2], g_ffn.unsqueeze(0).partition_broadcast(P)).then_inc(g_in, 16)

            def weights():
                for w_s, w in ((wq_s, wq_t), (wk_s, wk_t), (wv_s, wv_t), (wo_s, wo_t), (wr_s, wr)):
                    sp.dma_start(w_s[:, :], w).then_inc(w_in, 16)
                sp.dma_start(br_s[:, :], br.unsqueeze(0).partition_broadcast(P)).then_inc(w_in, 16)
                sp.wait_ge(kb_ready, 1)
                sp.dma_start(kb_dram, kb_s[:, :]).then_inc(kb_out, 16)
                sp.wait_ge(kb_out, 16)

            def tick(p, a, b, c, d, on):
                in_p, in_a, in_b, in_c, in_d = on
                if in_p:
                    wait_apart(sp, lna, p.minus(2).count(7, 7), sp_passed)
                    sp.dma_start(x_in[:, p.par, :, :], x_t[bass.ds(p.num(), 1)].rearrange("o p j d -> p (o j) d")
                                 ).then_inc(x_got[p.par], 16)
                    wait_apart(sp, v_ps, p.minus(2).count(1, 1), sp_passed)
                    sp.dma_start(ctx_in[:, p.par, :], ctx_t[bass.ds(p.num(), 1)].rearrange("o d l -> d (o l)")
                                 ).then_inc(ctx_got[p.par], 16)
                if in_c:
                    wait_apart(sp, m_sb, c.count(2, 2), sp_passed)
                    sp.dma_start(qk[c.par][SROWS:TROWS, 8:16, 0:L], m3_t[:, 1, :]).then_inc(m_in[1][c.par], 16)
                    wait_apart(sp, x2_ready, c.minus(2).count(1, 1), sp_passed)
                    sp.dma_start(x_res[:, c.par, :, :], x_t[bass.ds(c.num(), 1)].rearrange("o p j d -> p (o j) d")
                                 ).then_inc(res_got[c.par], 16)
                    wait_apart(sp, cxf, c.minus(2).count(2, 2), sp_passed)
                    if isinstance(c.i, int) and c.k == 0:
                        sp.wait_ge(vmean_sb, 1)
                        sp.dma_start(vm_dram, vmean[:, :]).then_inc(vmean_out, 16)
                        sp.wait_ge(vmean_out, 16)
                    sp.dma_start(vm_in[:, c.par, :], vm_dram[bass.ds(c.num(), 1), :].partition_broadcast(P)
                                 ).then_inc(res_got[c.par], 16)
                if in_a:
                    wait_apart(sp, qk_mid, a.count(1, 1), sp_passed)
                    wait_apart(sp, qk_lo, a.count(1, 1), sp_passed)
                    pa = parts[:, a.par, :, :]
                    dst = qk_dram[a.par]
                    for hf in range(2):
                        wait_apart(sp, stack_in[hf][a.par], a.minus(2).landed(2), sp_passed)
                    put = parts_out[a.par]
                    sp.dma_start(dst[:, 0:2, :], pa[:, 0:2, :]).then_inc(put, 16)
                    sp.dma_start(dst[:, 2:4, 0:L], pa[:, 0:1, 0:L].to_broadcast([P, 2, L])).then_inc(put, 16)
                    sp.dma_start(dst[:, 2:4, L:2 * L], pa[:, 1:3, L:2 * L]).then_inc(put, 16)
                    sp.dma_start(dst[:, 4:6, 0:L], pa[:, 1:3, 0:L]).then_inc(put, 16)
                    sp.dma_start(dst[:, 4:6, L:2 * L], pa[:, 0:1, L:2 * L].to_broadcast([P, 2, L])).then_inc(put, 16)
                    wait_apart(sp, put, a.landed(5), sp_passed)

                def stack_half(hf):
                    wait_apart(sp, t_made, a.minus(2).count(LOADS, (hf + 1) * LOADS // 2), sp_passed)
                    if isinstance(a.i, int) and a.k < 2:
                        sp.wait_ge(vconst, 12)
                    sp.dma_start(qk[a.par][0:KROWS, 8 * hf:8 * hf + 8, :],
                                 qk_dram[a.par].rearrange("(h d) j q -> (d j) h q", d=DH)[:, 8 * hf:8 * hf + 8, :]
                                 ).then_inc(stack_in[hf][a.par], 16)
                    sp.dma_start(qk[a.par][KROWS:SROWS, 8 * hf:8 * hf + 8, L:2 * L],
                                 kb_dram[bass.ds(a.num(), 1), :].unsqueeze(1).to_broadcast([1, 8, L])
                                 ).then_inc(stack_in[hf][a.par], 16)

                if in_a:
                    stack_half(0)
                if in_b:
                    wait_apart(sp, m_sb, b.count(2, 1), sp_passed)
                    sp.dma_start(qk[b.par][SROWS:TROWS, 0:8, 0:L], m3_t[:, 0, :]).then_inc(m_in[0][b.par], 16)
                if in_d:
                    wait_apart(sp, x2_ready, d.count(1, 1), sp_passed)
                    sp.dma_start(out_t[bass.ds(d.num(), 1)].rearrange("o p j d -> p (o j) d"),
                                 rows[:, d.par, :, D:2 * D]).then_inc(x2_out[d.par], 16)
                if in_a:
                    stack_half(1)

            first = [True]

            def tick0(*args):
                tick(*args)
                if first[0]:
                    weights()
                    sp.wait_ge(vconst, 6)
                    sp.dma_start(rows_dram.rearrange("(p c) w -> p c w", p=P),
                                 filler[:, :].unsqueeze(1).to_broadcast([P, N // P, RW])).then_inc(fill_out, 16)
                first[0] = False

            ticks(sp, tick0)

            for par in range(2):
                wait_apart(sp, sent[par], Batch(0, B - 2 + par).landed(NQ), sp_passed)

            def expert(e):
                if not (isinstance(e.i, int) and e.k < 2):
                    wait_apart(sp, eo, e.minus(2).count(2 + CC, 2 + CC), sp_passed)
                n = e.num()
                one = bass.ds(n, 1)
                sp.dma_start(er[:, e.par, :, :], rows_dram.rearrange("(e c p) w -> e p c w", e=E, p=P)[one]
                             .rearrange("o p c w -> p (o c) w")).then_inc(er_in[e.par], 16)
                sp.dma_start(w1_s[:, e.par, :], w1[one].rearrange("o a b -> a (o b)")).then_inc(ew_in[e.par], 16)
                sp.dma_start(w2_s[:, e.par, :], w2[one].rearrange("o a b -> a (o b)")).then_inc(ew_in[e.par], 16)
                sp.dma_start(b1_s[:, e.par, :], b1[one].rearrange("o a b -> a (o b)")).then_inc(ew_in[e.par], 16)
                sp.dma_start(b2_s[:, e.par, :], b2[one, :].partition_broadcast(P)).then_inc(ew_in[e.par], 16)

            experts(sp, expert)

        @block.gpsimd
        def _(pool):
            pool.memset(ident[:, :], 0.0).then_inc(const_base, 1)
            pool.memset(ident_b[:, :], 0.0).then_inc(const_base, 1)
            pool.memset(causal[:, :], 0.0).then_inc(const_base, 1)
            pool.memset(tri[:, :], 1.0).then_inc(const_base, 1)
            pool.wait_ge(const_base, 4)
            for m in (ident, ident_b):
                pool.affine_select(out=m[:, :], in_=m[:, :], compare_op=ALU.not_equal, fill=1.0, base=0,
                                   pattern=[[-1, P]], channel_multiplier=1).then_inc(const_ready, 1)
            pool.affine_select(out=causal[:, :], in_=causal[:, :], compare_op=ALU.is_ge, fill=NEG, base=0,
                               pattern=[[-1, P]], channel_multiplier=1).then_inc(const_ready, 1)
            pool.affine_select(out=tri[:, :], in_=tri[:, :], compare_op=ALU.is_ge, fill=0.0, base=0,
                               pattern=[[1, P]], channel_multiplier=-1).then_inc(const_ready, 1)
            for e in range(E):
                pool.memset(rank[:, :, e:e + 1], float(E - e)).then_inc(const_base, 1)
                pool.memset(slot0[:, :, e:e + 1], float(C * e)).then_inc(const_base, 1)
            pool.iota(token[:, :], [[P, NQ]], base=0, channel_multiplier=1,
                      allow_small_or_imprecise_dtypes=True).then_inc(const_ready, 1)

            pool.memset(ctx_sum[:, :, :], 0.0).then_inc(const_base, 1)
            pool.memset(ctx_all[:, FULL, :], 0.0).then_inc(const_base, 1)
            pool.wait_ge(const_base, 4 + 2 * E + 2)
            pool.wait_ge(dead_found, 2)
            found = pool.value_load(any_dead[0:1, 0:1])
            with pool.If(found):
                with pool.Fori(0, B) as i:
                    pool.dma_start(ctx_all[:, 0:FULL, :], ctx[bass.ds(i, 1), 0:FULL * P, :]
                                   .rearrange("o (p c) d -> p (o c) d", c=FULL)).then_inc(all_in, 16)
                    pool.dma_start(ctx_all[0:REST, FULL, :], ctx[bass.ds(i, 1), FULL * P:LK, :]
                                   .rearrange("o p d -> p (o d)")).then_inc(all_in, 16)
                    wait_apart(pool, all_in, i * 32 + 32, pool_passed)
                    for n in range(FULL + 1):
                        one = ctx_sum[:, bass.ds(i, 1), :]
                        pool.tensor_tensor(one, one, ctx_all[:, n:n + 1, :], ALU.add).then_inc(all_add, 1)
                        wait_apart(pool, all_add, i * (FULL + 1) + (n + 1), pool_passed)
            pool.memset(mark[:, :], 0.0).then_inc(csum_ready, 1)

            def tick(p, a, b, c, d, on):
                in_p, in_a, in_b, in_c, in_d = on

                def mask_far(quad):
                    wait_apart(pool, t_exp, c.count(LOADS, 3 * quad + 2), pool_passed)
                    v = pt[:, quad % 2, 0:4 * L].rearrange("p (h q) -> p h q", q=L)[:, :, 0:P]
                    pool.affine_select(out=v, in_=v, compare_op=ALU.is_ge, fill=0.0, base=0,
                                       pattern=[[0, 4], [1, P]], channel_multiplier=-1).then_inc(t_masked, 1)

                def mask_near(quad):
                    wait_apart(pool, t_exp, c.count(LOADS, 3 * quad + 3), pool_passed)
                    v = pt[:, quad % 2, 4 * L:4 * (L + P)].rearrange("p (h q) -> p h q", q=P)
                    pool.affine_select(out=v, in_=v, compare_op=ALU.is_ge, fill=0.0, base=0,
                                       pattern=[[0, 4], [1, P]], channel_multiplier=-1).then_inc(t_masked, 1)

                if in_c:
                    mask_far(0)
                    mask_near(0)
                if in_a:
                    pool.wait_ge(qk_mid, a.count(1, 1))
                    wait(pool, parts_out[a.par], a.minus(2).landed(5))
                    pool.tensor_tensor(parts[:, a.par, 2, :], resid[:, :], parts[:, a.par, 1, :], ALU.subtract
                                       ).then_inc(qk_lo, 1)
                if in_c:
                    mask_far(1)
                    mask_near(1)
                if in_c:
                    mask_far(2)
                if in_d:
                    pool.wait_ge(lnb, d.count(7, 5))
                    pool.tensor_tensor(lnb_rs[:, :], lnb_ve[:, :], half[:, :], ALU.pow).then_inc(lnb_pow, 1)
                if in_c:
                    mask_near(2)
                if in_p:
                    pool.wait_ge(lna, p.count(7, 5))
                    pool.tensor_tensor(lna_rs[:, :], lna_ve[:, :], half[:, :], ALU.pow).then_inc(lna_pow, 1)
                if in_c:
                    mask_far(3)
                    mask_near(3)
                if in_d:
                    wait_apart(pool, rs, d.count(15, 15), pool_passed)
                    if isinstance(d.i, int) and d.k == 0:
                        pool.wait_ge(fill_out, 16)
                    for j in range(NQ):
                        pool.indirect_dma_start(
                            out=rows_dram, out_offset=bass.IndirectOffsetOnAxis(ap=slot_i[:, d.par, j:j + 1], axis=0),
                            in_=rows[:, d.par, j, :], in_offset=None, bounds_check=N - 1, oob_is_err=False,
                        ).then_inc(sent[d.par], 16)

            ticks(pool, tick)

            for par in range(2):
                pool.wait_ge(x2_out[par], Batch(0, B - 2 + par).landed(1))
                pool.wait_ge(sent[par], Batch(0, B - 2 + par).landed(NQ))

            def expert(e):
                wait_apart(pool, eo, e.count(2 + CC, 2 + CC), pool_passed)
                for j in range(CC):
                    pool.indirect_dma_start(
                        out=out_rows, out_offset=bass.IndirectOffsetOnAxis(ap=e_tok[:, e.par, j:j + 1], axis=0),
                        in_=e_out[:, e.par, j, :], in_offset=None, bounds_check=N - 1, oob_is_err=False,
                    ).then_inc(eo_out[e.par], 16)

            experts(pool, expert)
            for par in range(2):
                pool.wait_ge(eo_out[par], Batch(0, E - 2 + par).landed(CC))

        @block.scalar
        def _(act):
            act.wait_ge(g_in, 32)
            act.activation(tg[:, :], gates[:, :], ACT.Tanh).then_inc(tg_ready, 1)

            def means():
                act.wait_ge(csum_ps, 1)
                act.activation(csum_t[:, :], mb[:, 0:B], ACT.Copy).then_inc(csum_sb, 1)
                act.wait_ge(vmean_ps, 1)
                act.activation(vmean[:, :], mb[0:B, 0:D], ACT.Copy).then_inc(vmean_sb, 1)

            def tick(p, a, b, c, d, on):
                in_p, in_a, in_b, in_c, in_d = on

                def exp(i):
                    if not in_c:
                        return
                    quad = i // 3
                    if i % 3 == 0:
                        wait(act, pv, c.count(QUADS, quad - 1))
                    act.wait_ge(t_made, c.count(LOADS, i + 1))
                    act.activation(pt[:, quad % 2, 512 * (i % 3):512 * (i % 3) + 512], t_ps[i % 3][:, :], ACT.Exp,
                                   scale=SCALE).then_inc(t_exp, 1)

                exp(0)
                if in_c:
                    act.wait_ge(m_ps, c.count(2, 2))
                    wait(act, m_in[1][1 - c.par], c.minus(1).landed(1))
                    act.activation(m3_t[:, 1, :], ma_b[0:24, 0:L], ACT.Copy).then_inc(m_sb, 1)
                if in_a:
                    act.wait_ge(xt_ps, a.count(1, 1))
                    wait(act, qk_ps, a.count(1, 0))
                    act.activation(xn_t[:, :], mb[:, 0:L], ACT.Copy).then_inc(xt_sb, 1)
                exp(1)
                if in_b:
                    act.wait_ge(v_ps, b.count(1, 1))
                    wait(act, pv, b.minus(2).count(QUADS, QUADS))
                    if isinstance(b.i, int) and b.k == 0:
                        act.wait_ge(vconst, 12)
                    for j in range(NQ):
                        for sub in range(2):
                            dst = v_aug[:, b.par, j, :, :].rearrange("p (n s) w -> p n s w", s=2)[:, :, sub,
                                                                                                HW * sub:HW * sub + DH]
                            src = ma[:, j * D:(j + 1) * D].rearrange("p (n s d) -> p n s d", s=2, d=DH)[:, :, sub, :]
                            act.activation(dst, src, ACT.Copy).then_inc(v_sb, 1)
                exp(2)
                if in_d:
                    act.wait_ge(pv, d.count(QUADS, QUADS))
                    wait(act, o_turned, d.count(1, 0))
                    act.activation(o_sb[:, :], o_ps[:, :], ACT.Copy).then_inc(o_copied, 1)
                if in_a:
                    act.wait_ge(qk_ps, a.count(1, 1))
                    wait(act, parts_out[a.par], a.minus(2).landed(5))
                    act.activation(parts[:, a.par, 0, :], mb[:, :], ACT.Copy).then_inc(qk_hi, 1)
                exp(3)
                if in_a:
                    act.wait_ge(qk_res, a.count(1, 1))
                    act.activation(parts[:, a.par, 1, :], resid[:, :], ACT.Copy).then_inc(qk_mid, 1)
                exp(4)
                exp(5)
                if in_d:
                    act.wait_ge(cx_ps, d.count(1, 1))
                    wait(act, at_ps, d.count(1, 0))
                    act.activation(cx_t[:, :], mb[:, 0:L], ACT.Copy).then_inc(cx_sb, 1)
                exp(6)
                exp(7)
                if in_b:
                    act.wait_ge(m_ps, b.count(2, 1))
                    wait(act, m_in[0][1 - b.par], b.minus(1).landed(1))
                    act.activation(m3_t[:, 0, :], mb_b[0:24, 0:L], ACT.Copy).then_inc(m_sb, 1)
                exp(8)
                if in_d:
                    act.wait_ge(x2t_ps, d.count(1, 1))
                    wait(act, lg_ps, d.count(1, 0))
                    act.activation(x2n_t[:, :], ma[:, 0:L], ACT.Copy).then_inc(x2t_sb, 1)
                exp(9)
                exp(10)
                if in_d:
                    act.wait_ge(rt, d.count(6, 3))
                    act.activation(lg_e[:, :, :], lg_d[:, :, :], ACT.Exp).then_inc(e_ready, 1)
                exp(11)

            ticks(act, tick, means)

            def expert(e):
                act.wait_ge(ei_ps, e.count(1, 1))
                wait(act, eh_ps, e.count(1, 0))
                act.activation(e_in_t[:, :], s_ps[0][:, :], ACT.Copy).then_inc(ei_sb, 1)
                act.wait_ge(eh_ps, e.count(1, 1))
                wait(act, eo_ps, e.count(1, 0))
                act.wait_ge(ew_in[e.par], e.landed(4))
                act.activation(e_h[:, :], s_ps[1][:, :], ACT.Relu, bias=b1_s[:, e.par, :]).then_inc(eh_sb, 1)

            experts(act, expert)

        @block.vector
        def _(dve):
            dve.memset(filler[:, :], FAR).then_inc(vconst, 1)
            dve.memset(half[:, :], -0.5).then_inc(vconst, 1)
            dve.memset(ones_b[:, :], 1.0).then_inc(vconst, 1)
            dve.memset(mean_w[:, :], 1.0 / LK).then_inc(vconst, 1)
            dve.memset(carry[:, :, :], 0.0).then_inc(vconst, 1)
            dve.memset(v_aug[:, :, :, :, :], 0.0).then_inc(vconst, 1)
            dve.wait_ge(mask0_in, 16)
            dve.tensor_scalar(no_key[:, :], mask0[:, :], 0, None, ALU.is_equal).then_inc(dead_found, 1)
            dve.wait_ge(dead_found, 1)
            dve.tensor_reduce(any_dead[:, :], no_key[:, :], AX_X, ALU.max).then_inc(dead_found, 1)
            dve.wait_ge(mask_in, 16)
            dve.tensor_scalar(kb_s[:, :], mask_s[:, :], 0, NEG, ALU.is_equal, ALU.mult).then_inc(kb_ready, 1)
            dve.wait_ge(vconst, 6)
            for sub in range(2):
                for par in range(2):
                    v = v_aug[:, par, :, :, :].rearrange("p j (n s) w -> p (j n) s w", s=2)[:, :, sub,
                                                                                         HW * sub + DH:HW * sub + DH + 1]
                    dve.memset(v, 1.0).then_inc(vconst, 1)
            for q in qk:
                dve.memset(q[:, :, :], 1.0).then_inc(vconst, 1)

            def norm(ch, src, stats, mv, ve, rstd, powd, batch, dst):
                def first():
                    for j in range(NQ):
                        ch.did(dve.bn_stats(stats[:, j, :], src[:, j, :]))
                    wait_apart(dve, ch.sem, batch.count(ch.per, ch.n), dve_passed)
                    for j in range(NQ):
                        ch.did(dve.bn_aggr(mv[:, j, :], stats[:, j, :]))
                    ch.settle()
                    ch.did(dve.tensor_scalar(ve[:, :], mv[:, :, 1], EPS, None, ALU.add))

                def second():
                    dve.wait_ge(powd, batch.count(1, 1))
                    for j in range(NQ):
                        ch.did(dve.tensor_scalar(dst[:, j, :], src[:, j, :], mv[:, j, 0:1], rstd[:, j:j + 1],
                                                 ALU.subtract, ALU.mult))
                return first, second

            def tick(p, a, b, c, d, on):
                in_p, in_a, in_b, in_c, in_d = on

                def reduce_max(i):
                    if not in_b:
                        return
                    dve.wait_ge(s_made, b.count(LOADS, i + 1))
                    hs = heads(i // 3)
                    v = s_ps[i % 2][:, :]
                    if i % 3 < 2:
                        lo = hs[2 * (i % 3)]
                        o, v = max_far[:, lo:lo + 3:2, :], v.rearrange("p (h s k) -> p h s k", s=2, k=P)
                    else:
                        o, v = max_near[:, hs[0]:hs[0] + 7:2], v.rearrange("p (h k) -> p h k", k=P)
                    dve.tensor_reduce(o, v, AX_X, ALU.max).then_inc(s_max, 1)

                def split_max(hf):
                    ch = Steps(dve, mch, b, 15, 8 * hf)
                    h8 = slice(8 * hf, 8 * hf + 8)
                    dve.wait_ge(s_max, b.count(LOADS, (hf + 1) * LOADS // 2))
                    wait(dve, m_ps, b.minus(1).count(2, hf + 1))
                    ch.did(dve.tensor_tensor(max_tmp[:, :], max_far[:, h8, 0], max_far[:, h8, 1], ALU.max))
                    ch.settle()
                    ch.did(dve.tensor_scalar(neg_max[:, 1, :], max_tmp[:, :], MAX_FLOOR, -1.0, ALU.max, ALU.mult))
                    ch.did(dve.tensor_scalar(neg_max[:, 0, :], max_near[:, h8], MAX_FLOOR, -1.0, ALU.max, ALU.mult))
                    ch.settle()
                    m = m3[:, hf, :, :, :]
                    ch.did(dve.tensor_copy(m[:, :, 0, :], neg_max[:, :, :]))
                    ch.settle()
                    ch.did(dve.tensor_tensor(neg_res[:, :, :], neg_max[:, :, :], m[:, :, 0, :], ALU.subtract))
                    ch.settle()
                    ch.did(dve.tensor_copy(m[:, :, 1, :], neg_res[:, :, :]))
                    ch.settle()
                    ch.did(dve.tensor_tensor(m[:, :, 2, :], neg_res[:, :, :], m[:, :, 1, :], ALU.subtract))
                    if hf == 0:
                        wait(dve, cxf, b.minus(2).count(2, 2))
                        ch.did(dve.tensor_scalar(dead[:, b.par, :, :], neg_max[:, :, 0:1], DEAD_AT, None, ALU.is_ge))

                if in_p:
                    lna_1, lna_2 = norm(Steps(dve, lna, p, 7), x_in[:, p.par, :, :], lna_st, lna_mv, lna_ve, lna_rs,
                                        lna_pow, p, xn[:, p.par, :, :])
                if in_d:
                    x2 = rows[:, d.par, :, D:2 * D]
                    lnb_1, lnb_2 = norm(Steps(dve, lnb, d, 7), x2, lnb_st, lnb_mv, lnb_ve, lnb_rs, lnb_pow, d, x2n)

                reduce_max(0)
                reduce_max(1)
                reduce_max(2)
                if in_a:
                    dve.wait_ge(qk_hi, a.count(1, 1))
                    wait(dve, qk_lo, a.count(1, 0))
                    dve.tensor_tensor(resid[:, :], mb[:, :], parts[:, a.par, 0, :], ALU.subtract).then_inc(qk_res, 1)
                reduce_max(3)
                reduce_max(4)
                if in_d:
                    ch = Steps(dve, cxn, d, 3)
                    dve.wait_ge(o_turned, d.count(1, 1))
                    o = ma[:, :].rearrange("p (j h w) -> p j h w", j=NQ, w=HW)
                    ch.did(dve.tensor_tensor(l_sum[:, :, :], o[:, :, :, DH],
                                             dead[:, d.par, :, :].to_broadcast([P, NQ, H]), ALU.add))
                    ch.settle()
                    ch.did(dve.reciprocal(l_inv[:, :, :], l_sum[:, :, :]))
                    ch.settle()
                    wait(dve, cxf, d.count(2, 0))
                    ch.did(dve.tensor_tensor(cx_n[:, :, :, :], o[:, :, :, 0:DH],
                                             l_inv[:, :, :].unsqueeze(3).to_broadcast([P, NQ, H, DH]), ALU.mult))
                    ch.settle()
                    dve.wait_ge(res_got[d.par], d.landed(2))
                    wait(dve, cx_ps, d.count(1, 0))
                    for j in range(NQ):
                        dve.scalar_tensor_tensor(
                            out=cx_f[:, j, :], in0=vm_in[:, d.par, :], scalar=dead[:, d.par, j, :],
                            in1=cx_n[:, j, :, :].rearrange("p h d -> p (h d)"), op0=ALU.mult, op1=ALU.add
                        ).then_inc(cxf, 1)
                reduce_max(5)
                if in_b:
                    split_max(0)
                reduce_max(6)
                if in_d:
                    dve.wait_ge(at_ps, d.count(1, 1))
                    dve.wait_ge(res_got[d.par], d.landed(2))
                    if isinstance(d.i, int) and d.k == 0:
                        dve.wait_ge(tg_ready, 1)
                    wait(dve, sent[d.par], d.minus(2).landed(NQ))
                    wait(dve, x2_out[d.par], d.minus(2).landed(1))
                    dve.scalar_tensor_tensor(out=x2, in0=ma[:, 0:L].rearrange("p (j d) -> p j d", d=D),
                                             scalar=tg[:, 0:1], in1=x_res[:, d.par, :, :], op0=ALU.mult,
                                             op1=ALU.add).then_inc(x2_ready, 1)
                    dve.wait_ge(x2_ready, d.count(1, 1))
                    lnb_1()
                reduce_max(7)
                if in_d:
                    wait(dve, x2t_ps, d.count(1, 0))
                    lnb_2()
                reduce_max(8)
                if in_p:
                    dve.wait_ge(x_got[p.par], p.landed(1))
                    lna_1()
                reduce_max(9)
                if in_d:
                    ch = Steps(dve, rt, d, 6)
                    dve.wait_ge(lg_ps, d.count(1, 1))
                    if isinstance(d.i, int) and d.k == 0:
                        dve.wait_ge(w_in, 96)
                        dve.wait_ge(const_base, 4 + 2 * E)
                    ch.did(dve.tensor_tensor(lg[:, :, :], mb[:, 0:NQ * E].rearrange("p (j e) -> p j e", e=E),
                                             br_s[:, :].unsqueeze(1).to_broadcast([P, NQ, E]), ALU.add))
                    ch.settle()
                    ch.did(dve.tensor_reduce(lg_max[:, :], lg[:, :, :], AX_X, ALU.max))
                    ch.settle()
                    wait(dve, e_ready, d.count(1, 0))
                    ch.did(dve.tensor_tensor(lg_d[:, :, :], lg[:, :, :],
                                             lg_max[:, :].unsqueeze(2).to_broadcast([P, NQ, E]), ALU.subtract))
                    ch.settle()
                    ch.did(dve.scalar_tensor_tensor(out=w_rank[:, :, :], in0=lg_d[:, :, :], scalar=0.0,
                                                    in1=rank[:, :, :].to_broadcast([P, NQ, E]),
                                                    op0=ALU.is_ge, op1=ALU.mult))
                    ch.settle()
                    ch.did(dve.tensor_reduce(w_best[:, :], w_rank[:, :, :], AX_X, ALU.max))
                    ch.settle()
                    wait(dve, cum_ps, d.count(1, 0))
                    ch.did(dve.tensor_tensor(onehot[:, :, :], w_rank[:, :, :],
                                             w_best[:, :].unsqueeze(2).to_broadcast([P, NQ, E]), ALU.is_equal))
                if in_p:
                    wait(dve, xt_ps, p.count(1, -1))
                    lna_2()
                reduce_max(10)
                if in_d:
                    ch = Steps(dve, rs, d, 15)
                    ro = rows[:, d.par, :, :]
                    dve.wait_ge(e_ready, d.count(1, 1))
                    ch.did(dve.tensor_reduce(e_sum[:, :], lg_e[:, :, :], AX_X, ALU.add))
                    ch.settle()
                    ch.did(dve.reciprocal(gate[:, :], e_sum[:, :]))
                    ch.settle()
                    for j in range(NQ):
                        ch.did(dve.tensor_scalar(ro[:, j, 0:D], x2n[:, j, :], gate[:, j:j + 1], None, ALU.mult))
                    ch.did(dve.tensor_scalar(ro[:, :, 2 * D], gate[:, :], tg[:, 1:2], None, ALU.mult))
                    if isinstance(d.i, int) and d.k == 0:
                        dve.wait_ge(const_ready, 5)
                    ch.did(dve.tensor_copy(ro[:, :, 2 * D + 1], token[:, :]))
                    ch.settle()
                    ch.did(dve.tensor_scalar(token[:, :], token[:, :], float(L), None, ALU.add))
                reduce_max(11)
                if in_b:
                    split_max(1)
                if in_d:
                    dve.wait_ge(cum_ps, d.count(1, 1))
                    n = NQ * E
                    ch.did(dve.tensor_tensor(pos[:, :, :], mb[:, 0:n].rearrange("p (j e) -> p j e", e=E),
                                             carry[:, :, :].to_broadcast([P, NQ, E]), ALU.add))
                    ch.settle()
                    ch.did(dve.tensor_tensor(carry[:, 0, :], carry[:, 0, :], mb[:, n:n + E], ALU.add))
                    ch.did(dve.tensor_tensor(picked[:, 0:NQ, :], pos[:, :, :], onehot[:, :, :], ALU.mult))
                    ch.did(dve.tensor_tensor(picked[:, NQ:2 * NQ, :], onehot[:, :, :],
                                             slot0[:, :, :].to_broadcast([P, NQ, E]), ALU.mult))
                    ch.settle()
                    ch.did(dve.tensor_reduce(pick_sum[:, :], picked[:, :, :], AX_X, ALU.add))
                    ch.settle()
                    ch.did(dve.tensor_tensor(slot[:, :], pick_sum[:, 0:NQ], pick_sum[:, NQ:2 * NQ], ALU.add))
                    ch.did(dve.tensor_scalar(over[:, :], pick_sum[:, 0:NQ], float(C), FAR, ALU.is_ge, ALU.mult))
                    ch.settle()
                    ch.did(dve.tensor_tensor(slot_i[:, d.par, :], slot[:, :], over[:, :], ALU.add))

            ticks(dve, tick)

            def expert(e):
                ch = Steps(dve, eo, e, 2 + CC)
                wait(dve, eo, e.count(2 + CC, 0))
                dve.wait_ge(eo_ps, e.count(1, 1))
                dve.wait_ge(ew_in[e.par], e.landed(4))
                dve.wait_ge(er_in[e.par], e.landed(1))
                if not (isinstance(e.i, int) and e.k < 2):
                    dve.wait_ge(eo_out[e.par], e.minus(2).landed(CC))
                ch.did(dve.tensor_tensor(e_tmp[:, :, :], t_ps[0][:, :].rearrange("p (c d) -> p c d", d=D),
                                         b2_s[:, e.par, :].unsqueeze(1).to_broadcast([P, CC, D]), ALU.add))
                ch.did(dve.tensor_copy(e_tok[:, e.par, :], er[:, e.par, :, 2 * D + 1]))
                ch.settle()
                for j in range(CC):
                    ch.did(dve.scalar_tensor_tensor(out=e_out[:, e.par, j, :], in0=e_tmp[:, j, :],
                                                    scalar=er[:, e.par, j, 2 * D:2 * D + 1],
                                                    in1=er[:, e.par, j, D:2 * D], op0=ALU.mult, op1=ALU.add))

            experts(dve, expert)

        @block.tensor
        def _(pe):
            def means():
                pe.wait_ge(qk_res, 2)
                pe.wait_ge(m_sb, 1)
                pe.wait_ge(csum_ready, 1)
                pe.wait_ge(vconst, 12)
                for n in range(B):
                    last = pe.matmul(mb[:, n:n + 1], ctx_sum[:, n, :], mean_w[:, :], start=True, stop=True)
                last.then_inc(csum_ps, 1)
                pe.wait_ge(csum_sb, 1)
                pe.matmul(mb[0:B, 0:D], csum_t[:, :], wv_s[:, :], start=True, stop=True).then_inc(vmean_ps, 1)

            pe.wait_ge(vconst, 12)

            def tick(p, a, b, c, d, on):
                in_p, in_a, in_b, in_c, in_d = on

                def s_load(i):
                    if not in_b:
                        return
                    q = qk[b.par]
                    if i % (LOADS // 2) == 0:
                        pe.wait_ge(stack_in[i // (LOADS // 2)][b.par], b.landed(2))
                    wait(pe, s_max, b.count(LOADS, i - 1))
                    hs, bank = heads(i // 3), s_ps[i % 2]
                    if i % 3 < 2:
                        for n, h in enumerate(hs[2 * (i % 3):2 * (i % 3) + 2]):
                            pe.matmul(bank[:, L * n:L * n + L], q[0:SROWS, h, P:L], q[0:SROWS, h, L:2 * L],
                                      start=n == 0, stop=False, skip_group_check=True)
                        o = bank[:, :].rearrange("p (h s k) -> p h s k", s=2, k=P)[:, :, 1, :]
                        m = 2
                    else:
                        for n, h in enumerate(hs):
                            pe.matmul(bank[:, P * n:P * n + P], q[0:SROWS, h, 0:P], q[0:SROWS, h, L:L + P],
                                      start=n == 0, stop=False, skip_group_check=True)
                        o = bank[:, :].rearrange("p (h k) -> p h k", k=P)
                        m = 4
                    pe.matmul(o, ident_b[:, :], causal[:, :].unsqueeze(1).to_broadcast([P, m, P]), start=False,
                              stop=True, skip_group_check=True).then_inc(s_made, 1)

                def t_load(i):
                    if not in_c:
                        return
                    q = qk[c.par]
                    if i % (LOADS // 2) == 0:
                        pe.wait_ge(m_in[i // (LOADS // 2)][c.par], c.landed(1))
                    wait(pe, t_exp, c.count(LOADS, i - 2))
                    hs, bank = heads(i // 3), t_ps[i % 3]
                    if i % 3 < 2:
                        for n, h in enumerate(hs[2 * (i % 3):2 * (i % 3) + 2]):
                            last = pe.matmul(bank[:, L * n:L * n + L], q[0:TROWS, h, L:L + P], q[0:TROWS, h, 0:L],
                                             start=True, stop=True)
                    else:
                        for n, h in enumerate(hs):
                            last = pe.matmul(bank[:, P * n:P * n + P], q[0:TROWS, h, L + P:2 * L],
                                             q[0:TROWS, h, P:L], start=True, stop=True)
                    last.then_inc(t_made, 1)

                def values(bt, quad):
                    pe.wait_ge(t_exp, bt.count(LOADS, 3 * quad + 3))
                    pe.wait_ge(t_masked, bt.count(2 * QUADS, 2 * quad + 2))
                    if quad == 0:
                        pe.wait_ge(v_sb, bt.count(4, 4))
                        wait(pe, o_copied, bt.count(1, 0))
                    hf = quad // 2
                    for g, h in enumerate(heads(quad)):
                        pe.matmul(o_ps[32 * g:32 * g + 32, hf * L:hf * L + L], v_aug[:, bt.par, 0, h, :],
                                  pt[:, quad % 2, L * g:L * g + L], start=quad == 0, stop=False,
                                  skip_group_check=True)
                    for g, h in enumerate(heads(quad)):
                        last = pe.matmul(o_ps[32 * g:32 * g + 32, hf * L + P:hf * L + L], v_aug[:, bt.par, 1, h, :],
                                         pt[:, quad % 2, 4 * L + P * g:4 * L + P * g + P], start=False,
                                         stop=quad == QUADS - 1, skip_group_check=True)
                    last.then_inc(pv, 1)

                def turn_max(bt, hf, bank):
                    pe.wait_ge(mch, bt.count(15, 7 + 8 * hf))
                    for j in range(NQ):
                        last = pe.transpose(bank[0:24, j * P:j * P + P],
                                            m3[:, hf, j, :, :].rearrange("p a h -> p (a h)"), ident_b[:, :])
                    last.then_inc(m_ps, 1)

                s_load(0)
                t_load(0)
                if in_c:
                    pe.wait_ge(v_sb, c.count(4, 4))
                    wait(pe, x2t_sb, d.count(1, 0))
                    turn_max(c, 1, ma_b)
                if in_a:
                    wait(pe, rs, d.minus(1).count(15, 9))
                    if in_c:
                        pe.wait_ge(m_sb, c.count(2, 1))
                    wait(pe, qk_res, a.count(1, 0))
                    pe.wait_ge(lna, a.count(7, 7))
                    if isinstance(a.i, int) and a.k == 0:
                        pe.wait_ge(const_ready, 4)
                    if isinstance(a.i, int) and a.k == 2:
                        pe.wait_ge(vmean_sb, 1)
                    for j in range(NQ):
                        last = pe.transpose(mb[:, j * P:j * P + P], xn[:, a.par, j, :], ident[:, :])
                    last.then_inc(xt_ps, 1)
                s_load(1)
                t_load(1)
                if in_b:
                    wait(pe, m_sb, b.count(2, 0))
                    wait(pe, x2t_sb, d.count(1, 0))
                    for j in range(NQ):
                        last = pe.matmul(ma[:, j * D:(j + 1) * D], ctx_in[:, b.par, j * P:(j + 1) * P], wv_s[:, :],
                                         start=True, stop=True)
                    last.then_inc(v_ps, 1)
                if in_d:
                    values(d, QUADS - 1)
                s_load(2)
                t_load(2)
                if in_a:
                    if isinstance(a.i, int) and a.k == 0:
                        pe.wait_ge(w_in, 96)
                    pe.wait_ge(xt_sb, a.count(1, 1))
                    pe.wait_ge(ctx_got[a.par], a.landed(1))
                    pe.matmul(mb[:, 0:L], wq_s[:, :], xn_t[:, :], start=True, stop=True)
                    pe.matmul(mb[:, L:2 * L], wk_s[:, :], ctx_in[:, a.par, :], start=True, stop=True).then_inc(qk_ps, 1)
                s_load(3)
                t_load(3)
                if in_d:
                    if in_b:
                        pe.wait_ge(v_sb, b.count(4, 4))
                    elif in_c:
                        pe.wait_ge(m_sb, c.count(2, 2))
                    else:
                        pe.wait_ge(x2t_sb, d.count(1, 0))
                    pe.wait_ge(o_copied, d.count(1, 1))
                    for j in range(NQ):
                        for hf in range(2):
                            n = j * 2 + hf
                            last = pe.transpose(ma[:, n * P:n * P + P], o_sb[:, hf * L + j * P:hf * L + j * P + P],
                                                ident[:, :])
                    last.then_inc(o_turned, 1)
                s_load(4)
                t_load(4)
                if in_c:
                    values(c, 0)
                s_load(5)
                t_load(5)
                if in_d:
                    pe.wait_ge(cxf, d.count(2, 2))
                    if in_a:
                        pe.wait_ge(qk_res, a.count(1, 1))
                    wait(pe, rs, d.minus(1).count(15, 9))
                    for j in range(NQ):
                        last = pe.transpose(mb[:, j * P:j * P + P], cx_f[:, j, :], ident[:, :])
                    last.then_inc(cx_ps, 1)
                s_load(6)
                t_load(6)
                if in_d:
                    pe.wait_ge(cx_sb, d.count(1, 1))
                    for j in range(NQ):
                        last = pe.matmul(ma[:, j * D:(j + 1) * D], cx_t[:, j * P:(j + 1) * P], wo_s[:, :],
                                         start=True, stop=True)
                    last.then_inc(at_ps, 1)
                s_load(7)
                t_load(7)
                if in_b:
                    if in_a:
                        pe.wait_ge(qk_res, a.count(1, 1))
                    turn_max(b, 0, mb_b)
                if in_c:
                    values(c, 1)
                s_load(8)
                t_load(8)
                if in_d:
                    pe.wait_ge(lnb, d.count(7, 7))
                    for j in range(NQ):
                        last = pe.transpose(ma[:, j * P:j * P + P], x2n[:, j, :], ident[:, :])
                    last.then_inc(x2t_ps, 1)
                s_load(9)
                t_load(9)
                if in_d:
                    pe.wait_ge(x2t_sb, d.count(1, 1))
                    if in_b:
                        pe.wait_ge(m_sb, b.count(2, 1))
                    for j in range(NQ):
                        last = pe.matmul(mb[:, E * j:E * j + E], x2n_t[:, j * P:(j + 1) * P], wr_s[:, :],
                                         start=True, stop=True)
                    last.then_inc(lg_ps, 1)
                s_load(10)
                t_load(10)
                if in_c:
                    values(c, 2)
                s_load(11)
                t_load(11)
                if in_d:
                    pe.wait_ge(rt, d.count(6, 6))
                    n = NQ * E
                    for j in range(NQ + 1):
                        o = mb[:, E * j:E * j + E]
                        for jj in range(min(j + 1, NQ)):
                            last = pe.matmul(o, (tri if jj == j else ones_b)[:, :], onehot[:, jj, :],
                                             start=jj == 0, stop=jj == min(j, NQ - 1))
                    last.then_inc(cum_ps, 1)

            ticks(pe, tick, means)

            pe.wait_ge(s_max, LOADS * B)
            pe.wait_ge(t_exp, LOADS * B)

            def expert(e):
                pe.wait_ge(er_in[e.par], e.landed(1))
                wait(pe, ei_sb, e.count(1, 0))
                for j in range(CC):
                    last = pe.transpose(s_ps[0][:, j * P:j * P + P], er[:, e.par, j, 0:D], ident[:, :])
                last.then_inc(ei_ps, 1)
                pe.wait_ge(ei_sb, e.count(1, 1))
                pe.wait_ge(ew_in[e.par], e.landed(4))
                pe.matmul(s_ps[1][:, :], w1_s[:, e.par, :], e_in_t[:, :], start=True, stop=True).then_inc(eh_ps, 1)
                pe.wait_ge(eh_sb, e.count(1, 1))
                wait(pe, eo, e.minus(1).count(2 + CC, 1))
                for j in range(CC):
                    last = pe.matmul(t_ps[0][:, j * D:(j + 1) * D], e_h[:, j * P:(j + 1) * P], w2_s[:, e.par, :],
                                     start=True, stop=True)
                last.then_inc(eo_ps, 1)

            experts(pe, expert)


def kernel(x, ctx_1024, mask_BxS2_if1, g_xattn, g_ffn, L0_xattn_Wq, L0_xattn_Wk, L0_xattn_Wv, L0_xattn_Wo,
           L0_ffn_Wr, L0_ffn_br, L0_ffn_W1, L0_ffn_b1, L0_ffn_W2, L0_ffn_b2):
    import numpy as np
    import concourse.bacc as bacc
    from concourse.bass_utils import run_bass_kernel_spmd

    seen = x.shape[1]
    ctx = np.asarray(ctx_1024)
    b1 = np.asarray(L0_ffn_b1)
    laid = {
        "x": x, "ctx": ctx, "ctx_t": ctx[:, :seen, :].transpose(0, 2, 1), "mask": mask_BxS2_if1,
        "g_xattn": g_xattn, "g_ffn": g_ffn,
        "wq_t": np.asarray(L0_xattn_Wq).T, "wk_t": np.asarray(L0_xattn_Wk).T,
        "wv_t": np.asarray(L0_xattn_Wv).T, "wo_t": np.asarray(L0_xattn_Wo).T,
        "wr": L0_ffn_Wr, "br": L0_ffn_br, "w1": L0_ffn_W1, "b1": b1.reshape(*b1.shape, 1),
        "w2": L0_ffn_W2, "b2": L0_ffn_b2,
    }
    nc = bacc.Bacc("TRN2", target_bir_lowering=False, num_devices=1)
    arrays, args = {}, []
    for name, a in laid.items():
        a = np.ascontiguousarray(a)
        arrays[f"in_{name}"] = a
        args.append(nc.dram_tensor(f"in_{name}", a.shape, mybir.dt.from_np(a.dtype), kind="ExternalInput").ap())
    out = nc.dram_tensor("out_0", x.shape, F32, kind="ExternalOutput").ap()
    build(nc, *args, out)
    r = run_bass_kernel_spmd(nc, [arrays], core_ids=[0])
    return r.results[0]["out_0"]
```

```python
from contextlib import ExitStack

import concourse.bass as bass
from concourse import mybir

ALU = mybir.AluOpType
ACT = mybir.ActivationFunctionType
AX_X = mybir.AxisListType.X
F32 = mybir.dt.float32
BF16 = mybir.dt.bfloat16
I32 = mybir.dt.int32

P = 128
NEG = -1e30
MAX_FLOOR = -1e29
DEAD_AT = 5e28
FAR = 1.0e6
EPS = 1e-5
TWO_ONES = 1.0 + 127 / 2 ** 16


class Batch:

    def __init__(self, i, k):
        self.i, self.k = i, k
        self.par = k % 2

    def num(self):
        return self.i * 2 + self.k

    def minus(self, n):
        return Batch(self.i, self.k - n)

    def count(self, per, done):
        return self.i * (2 * per) + (self.k * per + done)

    def landed(self, dmas):
        return self.i * (16 * dmas) + (self.k // 2 + 1) * 16 * dmas


def wait(eng, sem, value):
    if not (isinstance(value, int) and value <= 0):
        eng.wait_ge(sem, value)


def wait_apart(eng, sem, value, passed):
    if isinstance(value, int):
        wait(eng, sem, value)
    else:
        eng.wait_ge(sem, value).then_inc(passed, 1)


class Steps:

    def __init__(self, eng, sem, batch, per, start=0):
        self.eng, self.sem, self.batch, self.per, self.n = eng, sem, batch, per, start

    def did(self, ins):
        ins.then_inc(self.sem, 1)
        self.n += 1
        assert self.n <= self.per

    def settle(self):
        self.eng.wait_ge(self.sem, self.batch.count(self.per, self.n))


def build(nc, x, ctx, ctx_t, mask, g_xattn, g_ffn, wq_t, wk_t, wv_t, wo_t, wr, br, w1, b1, w2, b2, out):
    B, L, D = x.shape
    LK = ctx.shape[1]
    E = wr.shape[1]
    H = 16
    DH = D // H
    N = B * L
    C = N // E
    NQ = L // P
    QUADS = H // 4
    LOADS = 3 * QUADS
    SCALE = float(DH) ** -0.5
    PARTS = 6
    KROWS = DH * PARTS
    SROWS = 96
    TROWS = SROWS + 3
    VW = 32
    HW = 16
    RW = 2 * D + 2
    CC = C // P
    FILLS = 4
    FULL = LK // P
    REST = LK - FULL * P
    assert D == P and L == 2 * P and N % E == 0

    x_t = x.rearrange("b (j p) d -> b p j d", p=P)
    out_t = out.rearrange("b (j p) d -> b p j d", p=P)
    out_rows = out.rearrange("b l d -> (b l) d")
    qk_dram = nc.dram_tensor("qk_parts", [2, P, PARTS, 2 * L], BF16, kind="Internal").ap()
    kb_dram = nc.dram_tensor("key_bias", [B, L], BF16, kind="Internal").ap()
    vm_dram = nc.dram_tensor("value_mean", [B, D], F32, kind="Internal").ap()
    rows_dram = nc.dram_tensor("expert_rows", [N, RW], F32, kind="Internal").ap()

    with ExitStack() as stack:
        def sb(name, shape, dt=F32):
            return stack.enter_context(nc.sbuf_tensor(name, shape, dt))

        def ps(name, shape, dt=F32):
            return stack.enter_context(nc.psum_tensor(name, shape, dt))

        def sem(name):
            return stack.enter_context(nc.semaphore(name))

        def sems(name, n=2):
            return [sem(f"{name}{i}") for i in range(n)]

        ident = sb("ident", [P, P])
        ident_b = sb("ident_b", [P, P], BF16)
        causal = sb("causal", [P, P], BF16)
        minus_b = sb("minus_b", [P, P], BF16)
        tri = sb("tri", [P, P], BF16)
        ones_b = sb("ones_b", [P, P], BF16)
        wq_s, wk_s, wv_s, wo_s = (sb(n, [P, D]) for n in ("wq_s", "wk_s", "wv_s", "wo_s"))
        wr_s = sb("wr_s", [P, E])
        br_s = sb("br_s", [P, E])
        gates = sb("gates", [P, 2])
        tg = sb("tg", [P, 2])
        rank = sb("rank", [P, 1, E])
        slot0 = sb("slot0", [P, 1, E])
        mean_w = sb("mean_w", [P, 1])
        zero = sb("zero", [P, 1])
        filler = sb("filler", [P, RW])
        mask_s = sb("mask_s", [B, L], I32)
        kb_s = sb("kb_s", [B, L], BF16)
        mask0 = sb("mask0", [1, B], I32)
        no_key = sb("no_key", [1, B])
        any_dead = sb("any_dead", [1, 1], I32)
        ctx_sum = sb("ctx_sum", [P, B, D])
        ctx_all = sb("ctx_all", [P, FULL + 1, D])
        csum_t = sb("csum_t", [P, B])
        vmean = sb("vmean", [B, D])
        mark = sb("mark", [1, 1])

        x_in = sb("x_in", [P, 2, NQ, D])
        ctx_in = sb("ctx_in", [P, 2, L])
        x_res = sb("x_res", [P, 2, NQ, D])
        vm_in = sb("vm_in", [P, 2, D])
        lna_st = sb("lna_st", [P, NQ, 6])
        lna_mv = sb("lna_mv", [P, NQ, 2])
        lna_ve = sb("lna_ve", [P, NQ])
        lna_rs = sb("lna_rs", [P, NQ])
        lna_nb = sb("lna_nb", [P, NQ])
        half = sb("half", [P, NQ])
        xn = sb("xn", [P, NQ, D])
        xn_t = sb("xn_t", [P, L])
        parts = sb("parts", [P, 2, 3, 2 * L], BF16)
        qk = [sb(f"qk{i}", [P, H, 2 * L], BF16) for i in range(2)]
        v_aug = sb("v_aug", [P, 2, NQ, H, VW])
        max_far = sb("max_far", [P, H, 2])
        max_near = sb("max_near", [P, H])
        max_tmp = sb("max_tmp", [P, 8])
        neg_max = sb("neg_max", [P, NQ, 8])
        neg_res = sb("neg_res", [P, NQ, 8])
        m3 = sb("m3", [P, 2, NQ, 3, 8], BF16)
        m3_t = sb("m3_t", [24, 2, L], BF16)
        dead = sb("dead", [P, 2, NQ, 1])
        pt = sb("pt", [P, 2, 4 * (L + P)])
        o_sb = sb("o_sb", [P, 2 * L])
        l_sum = sb("l_sum", [P, NQ, H])
        l_inv = sb("l_inv", [P, NQ, H])
        cx_n = sb("cx_n", [P, NQ, H, DH])
        cx_f = sb("cx_f", [P, NQ, D])
        cx_t = sb("cx_t", [P, L])
        rows = sb("rows", [P, 2, NQ, RW])
        lnb_st = sb("lnb_st", [P, NQ, 6])
        lnb_mv = sb("lnb_mv", [P, NQ, 2])
        lnb_ve = sb("lnb_ve", [P, NQ])
        lnb_rs = sb("lnb_rs", [P, NQ])
        lnb_nb = sb("lnb_nb", [P, NQ])
        x2n = sb("x2n", [P, NQ, D])
        x2n_t = sb("x2n_t", [P, L])
        lg = sb("lg", [P, NQ, E])
        lg_max = sb("lg_max", [P, NQ])
        lg_d = sb("lg_d", [P, NQ, E])
        lg_e = sb("lg_e", [P, NQ, E])
        e_sum = sb("e_sum", [P, NQ])
        gate = sb("gate", [P, NQ])
        w_rank = sb("w_rank", [P, NQ, E])
        w_best = sb("w_best", [P, NQ])
        onehot = sb("onehot", [P, NQ, E], BF16)
        carry = sb("carry", [P, 1, E])
        pos = sb("pos", [P, NQ, E])
        picked = sb("picked", [P, 2 * NQ, E])
        pick_sum = sb("pick_sum", [P, 2 * NQ])
        over = sb("over", [P, NQ])
        slot = sb("slot", [P, NQ])
        slot_i = sb("slot_i", [P, 2, NQ], I32)
        token = sb("token", [P, NQ])

        w1_s = sb("w1_s", [P, 2, D])
        w2_s = sb("w2_s", [P, 2, D])
        b1_s = sb("b1_s", [P, 2, 1])
        b2_s = sb("b2_s", [P, 2, D])
        e_in = sb("e_in", [P, 2, CC, D])
        e_rest = sb("e_rest", [P, 2, CC, RW - D])
        e_in_t = sb("e_in_t", [P, 2, C])
        e_h = sb("e_h", [P, 2, C])
        e_tmp = sb("e_tmp", [P, CC, D])
        e_out = sb("e_out", [P, 2, CC, D])
        e_tok = sb("e_tok", [P, 2, CC], I32)

        s_ps = [ps(f"s_ps{i}", [P, 512]) for i in range(2)]
        t_ps = [ps(f"t_ps{i}", [P, 512]) for i in range(2)]
        o_ps = ps("o_ps", [P, 512])
        ma = ps("ma", [P, 512])
        mb = ps("mb", [P, 512])
        mc = ps("mc", [P, 512])
        mc_b = mc[:, :].bitcast(BF16)

        ei_bank, eh_bank, eo_bank = s_ps, t_ps, [ma, mb]

        w_in = sem("weights_in")
        g_in = sem("gates_in")
        mask_in = sem("mask_in")
        mask0_in = sem("mask0_in")
        kb_ready = sem("key_bias_ready")
        kb_out = sem("key_bias_out")
        fill_out = sem("filler_out")
        const_base = sem("const_base")
        const_ready = sem("const_ready")
        vconst = sem("vector_consts")
        fill_set = sem("filler_set")
        qk_ones = sems("stack_ones")
        v_zero = sem("value_zeros")
        v_ones = sem("value_ones")
        tg_ready = sem("tanh_ready")
        dead_found = sem("dead_found")
        all_in = sem("all_ctx_in")
        all_add = sem("all_ctx_added")
        csum_ready = sem("ctx_sum_ready")
        csum_ps = sem("ctx_sum_turned")
        csum_sb = sem("ctx_sum_copied")
        vmean_ps = sem("value_mean_made")
        vmean_sb = sem("value_mean_copied")
        vmean_out = sem("value_mean_out")

        sp_passed = sem("sp_passed")
        pool_passed = sem("pool_passed")
        dve_passed = sem("vector_passed")

        x_got = sems("x_got")
        ctx_got = sems("ctx_got")
        res_got = sems("residual_got")
        lna = sem("lna_steps")
        lna_pow = sem("lna_pow")
        xn_ready = sem("xn_ready")
        xt_ps = sem("xt_turned")
        xt_sb = sem("xt_copied")
        qk_ps = sem("qk_made")
        qk_sb = sem("qk_parts_made")
        parts_out = sems("parts_out")
        stack_in = [sems(f"stack_in{i}_") for i in range(2)]
        v_ps = sem("v_made")
        v_sb = sem("v_copied")
        s_made = sem("s_made")
        s_max = sem("s_max")
        mch = sem("max_steps")
        m_ps = sem("m_turned")
        m_sb = sem("m_copied")
        m_in = [sems(f"m_in{i}_") for i in range(2)]
        t_made = sem("t_made")
        t_exp = sem("t_exp")
        t_masked = sem("t_masked")
        pv = sem("pv_made")
        o_copied = sem("o_copied")
        o_turned = sem("o_turned")
        cxn = sem("cx_steps")
        cxf = sem("cx_fixed")
        cx_ps = sem("cx_turned")
        cx_sb = sem("cx_copied")
        at_ps = sem("attn_made")
        x2_ready = sem("x2_ready")
        x2_out = sems("x2_out")
        lnb = sem("lnb_steps")
        lnb_pow = sem("lnb_pow")
        x2n_ready = sem("x2n_ready")
        x2t_ps = sem("x2t_turned")
        x2t_sb = sem("x2t_copied")
        lg_ps = sem("logits_made")
        rt = sem("route_steps")
        e_ready = sem("exp_ready")
        cum_ps = sem("counts_made")
        gs = sem("gate_steps")
        gated = sem("gated_rows")
        rs = sem("row_steps")
        sent = sems("rows_sent")

        e1_in = sems("expert_w1_in")
        e2_in = sems("expert_w2_in")
        ex_in = sems("expert_inputs_in")
        er_in = sems("expert_rests_in")
        ei_ps = sem("expert_in_turned")
        ei_sb = sem("expert_in_copied")
        eh_ps = sem("expert_h_made")
        eh_sb = sem("expert_h_copied")
        eo_ps = sem("expert_out_made")
        eo = sem("expert_out_steps")
        eo_out = sems("expert_out_sent")

        def heads(quad):
            first = (quad // 2) * 8 + quad % 2
            return [first + 2 * g for g in range(4)]

        FIRST, LAST = 4, 14
        assert (LAST - FIRST) % 2 == 0

        def ticks(eng, tick, between=None, after_first=None):
            def run(i, k):
                t = Batch(i, k)
                known = isinstance(i, int)
                on = [not known or 0 <= k - n < B for n in (-2, -1, 0, 1, 2, 3, 4)]
                tick([t.minus(n) for n in (-2, -1, 0, 1, 2, 3, 4)], on)
            for k in range(-2, FIRST):
                run(0, k)
                if after_first and k == -2:
                    after_first()
                if between and k == -1:
                    between()
            with eng.Fori(0, (LAST - FIRST) // 2) as i:
                for k in range(2):
                    run(i, FIRST + k)
            for k in range(LAST, B + 4):
                run(0, k)

        def experts(eng, expert):
            for k in range(2):
                expert(Batch(0, k))
            with eng.Fori(0, (E - 2) // 2) as i:
                for k in range(2):
                    expert(Batch(i, 2 + k))

        def frame(eng, q, made):
            eng.memset(q[:, :, 0:L].bitcast(F32), TWO_ONES).then_inc(made, 1)
            eng.memset(q[0:SROWS, :, L:2 * L].bitcast(F32), 0.0).then_inc(made, 1)
            eng.wait_ge(made, 2)
            eng.memset(q[SROWS:P, :, L:2 * L].bitcast(F32), TWO_ONES).then_inc(made, 1)
            eng.wait_ge(made, 3)

        block = stack.enter_context(nc.Block())

        @block.sync
        def _(sp):
            with nc.allow_non_contiguous_dma(reason="one mask entry of each batch"):
                sp.dma_start(mask0[:, :], mask[:, 0:1].rearrange("b o -> o b")).then_inc(mask0_in, 16)
            sp.dma_start(mask_s[:, :], mask[:, 0:L]).then_inc(mask_in, 16)
            sp.dma_start(gates[:, 0:1], g_xattn.unsqueeze(0).partition_broadcast(P)).then_inc(g_in, 16)
            sp.dma_start(gates[:, 1:2], g_ffn.unsqueeze(0).partition_broadcast(P)).then_inc(g_in, 16)

            def weights():
                for w_s, w in ((wq_s, wq_t), (wk_s, wk_t), (wv_s, wv_t), (wo_s, wo_t), (wr_s, wr)):
                    sp.dma_start(w_s[:, :], w).then_inc(w_in, 16)
                sp.dma_start(br_s[:, :], br.unsqueeze(0).partition_broadcast(P)).then_inc(w_in, 16)
                sp.wait_ge(kb_ready, 1)
                sp.dma_start(kb_dram, kb_s[:, :]).then_inc(kb_out, 16)
                sp.wait_ge(kb_out, 16)

            def tick(batches, on):
                p, a, b, c, d, e, f = batches
                in_p, in_a, in_b, in_c, in_d, in_e, in_f = on

                def stack_half(hf):
                    wait_apart(sp, t_made, a.minus(2).count(LOADS, (hf + 1) * LOADS // 2), sp_passed)
                    if isinstance(a.i, int) and a.k < 2:
                        sp.wait_ge(qk_ones[a.k], 3)
                    sp.dma_start(qk[a.par][0:KROWS, 8 * hf:8 * hf + 8, :],
                                 qk_dram[a.par].rearrange("(h d) j q -> (d j) h q", d=DH)[:, 8 * hf:8 * hf + 8, :]
                                 ).then_inc(stack_in[hf][a.par], 16)
                    sp.dma_start(qk[a.par][KROWS:KROWS + 1, 8 * hf:8 * hf + 8, L:2 * L],
                                 kb_dram[bass.ds(a.num(), 1), :].unsqueeze(1).to_broadcast([1, 8, L])
                                 ).then_inc(stack_in[hf][a.par], 16)

                if in_p:
                    wait_apart(sp, xn_ready, p.minus(2).count(2, 2), sp_passed)
                    sp.dma_start(x_in[:, p.par, :, :], x_t[bass.ds(p.num(), 1)].rearrange("o p j d -> p (o j) d")
                                 ).then_inc(x_got[p.par], 16)
                    wait_apart(sp, v_ps, p.minus(2).count(1, 1), sp_passed)
                    sp.dma_start(ctx_in[:, p.par, :], ctx_t[bass.ds(p.num(), 1)].rearrange("o d l -> d (o l)")
                                 ).then_inc(ctx_got[p.par], 16)
                if in_c:
                    wait_apart(sp, x2_ready, c.minus(2).count(1, 1), sp_passed)
                    sp.dma_start(x_res[:, c.par, :, :], x_t[bass.ds(c.num(), 1)].rearrange("o p j d -> p (o j) d")
                                 ).then_inc(res_got[c.par], 16)
                    wait_apart(sp, cxf, c.minus(2).count(2, 2), sp_passed)
                    if isinstance(c.i, int) and c.k == 0:
                        sp.wait_ge(vmean_sb, 1)
                        sp.dma_start(vm_dram, vmean[:, :]).then_inc(vmean_out, 16)
                        sp.wait_ge(vmean_out, 16)
                    sp.dma_start(vm_in[:, c.par, :], vm_dram[bass.ds(c.num(), 1), :].partition_broadcast(P)
                                 ).then_inc(res_got[c.par], 16)
                    wait_apart(sp, m_sb, c.count(2, 2), sp_passed)
                    sp.dma_start(qk[c.par][SROWS:TROWS, 8:16, 0:L], m3_t[:, 1, :]).then_inc(m_in[1][c.par], 16)
                if in_a:
                    wait_apart(sp, qk_sb, a.count(3, 3), sp_passed)
                    pa = parts[:, a.par, :, :]
                    dst = qk_dram[a.par]
                    for hf in range(2):
                        wait_apart(sp, stack_in[hf][a.par], a.minus(2).landed(2), sp_passed)
                    put = parts_out[a.par]
                    sp.dma_start(dst[:, 0:2, :], pa[:, 0:2, :]).then_inc(put, 16)
                    sp.dma_start(dst[:, 2:4, 0:L], pa[:, 0:1, 0:L].to_broadcast([P, 2, L])).then_inc(put, 16)
                    sp.dma_start(dst[:, 2:4, L:2 * L], pa[:, 1:3, L:2 * L]).then_inc(put, 16)
                    sp.dma_start(dst[:, 4:6, 0:L], pa[:, 1:3, 0:L]).then_inc(put, 16)
                    sp.dma_start(dst[:, 4:6, L:2 * L], pa[:, 0:1, L:2 * L].to_broadcast([P, 2, L])).then_inc(put, 16)
                    wait_apart(sp, put, a.landed(5), sp_passed)
                    stack_half(0)
                if in_b:
                    wait_apart(sp, m_sb, b.count(2, 1), sp_passed)
                    sp.dma_start(qk[b.par][SROWS:TROWS, 0:8, 0:L], m3_t[:, 0, :]).then_inc(m_in[0][b.par], 16)
                if in_d:
                    wait_apart(sp, x2_ready, d.count(1, 1), sp_passed)
                    sp.dma_start(out_t[bass.ds(d.num(), 1)].rearrange("o p j d -> p (o j) d"),
                                 rows[:, d.par, :, D:2 * D]).then_inc(x2_out[d.par], 16)
                if in_a:
                    stack_half(1)

                if isinstance(b.i, int) and -1 <= b.k < FILLS - 1:
                    if b.k == -1:
                        sp.wait_ge(fill_set, 1)
                    rows_of = N // FILLS
                    sp.dma_start(rows_dram[(b.k + 1) * rows_of:(b.k + 2) * rows_of, :]
                                 .rearrange("(p c) w -> p c w", p=P),
                                 filler[:, :].unsqueeze(1).to_broadcast([P, rows_of // P, RW])).then_inc(fill_out, 16)

            ticks(sp, tick, after_first=weights)

            rows_v = rows_dram.rearrange("(e c p) w -> e p c w", e=E, p=P)

            def load_w1(e):
                one = bass.ds(e.num(), 1)
                sp.dma_start(w1_s[:, e.par, :], w1[one].rearrange("o a b -> a (o b)")).then_inc(e1_in[e.par], 16)
                sp.dma_start(b1_s[:, e.par, :], b1[one].rearrange("o a b -> a (o b)")).then_inc(e1_in[e.par], 16)

            def load_w2(e):
                one = bass.ds(e.num(), 1)
                sp.dma_start(w2_s[:, e.par, :], w2[one].rearrange("o a b -> a (o b)")).then_inc(e2_in[e.par], 16)
                sp.dma_start(b2_s[:, e.par, :], b2[one, :].partition_broadcast(P)).then_inc(e2_in[e.par], 16)

            def load_inputs(e):
                sp.dma_start(e_in[:, e.par, :, :], rows_v[bass.ds(e.num(), 1), :, :, 0:D]
                             .rearrange("o p c w -> p (o c) w")).then_inc(ex_in[e.par], 16)

            def load_rest(e):
                sp.dma_start(e_rest[:, e.par, :, :], rows_v[bass.ds(e.num(), 1), :, :, D:RW]
                             .rearrange("o p c w -> p (o c) w")).then_inc(er_in[e.par], 16)

            for k in range(2):
                load_w1(Batch(0, k))
                load_w2(Batch(0, k))
            for par in range(2):
                wait_apart(sp, sent[par], Batch(0, B - 2 + par).landed(NQ), sp_passed)

            def expert(e):
                first = isinstance(e.i, int) and e.k < 2
                if not first:
                    wait_apart(sp, ei_ps, e.minus(2).count(1, 1), sp_passed)
                load_inputs(e)
                if not first:
                    wait_apart(sp, eh_sb, e.minus(2).count(1, 1), sp_passed)
                    load_w1(e)
                    wait_apart(sp, eo, e.minus(2).count(2 + CC, 2 + CC), sp_passed)
                    load_w2(e)
                load_rest(e)

            experts(sp, expert)

        @block.gpsimd
        def _(pool):
            pool.memset(ident[:, :], 0.0).then_inc(const_base, 1)
            pool.memset(ident_b[:, :], 0.0).then_inc(const_base, 1)
            pool.memset(minus_b[:, :], 0.0).then_inc(const_base, 1)
            pool.memset(causal[:, :], 0.0).then_inc(const_base, 1)
            pool.memset(tri[:, :], 1.0).then_inc(const_base, 1)
            pool.wait_ge(const_base, 5)
            for m, one in ((ident, 1.0), (ident_b, 1.0), (minus_b, -1.0)):
                pool.affine_select(out=m[:, :], in_=m[:, :], compare_op=ALU.not_equal, fill=one, base=0,
                                   pattern=[[-1, P]], channel_multiplier=1).then_inc(const_ready, 1)
            pool.affine_select(out=causal[:, :], in_=causal[:, :], compare_op=ALU.is_ge, fill=NEG, base=0,
                               pattern=[[-1, P]], channel_multiplier=1).then_inc(const_ready, 1)
            pool.affine_select(out=tri[:, :], in_=tri[:, :], compare_op=ALU.is_ge, fill=0.0, base=0,
                               pattern=[[1, P]], channel_multiplier=-1).then_inc(const_ready, 1)
            for e in range(E):
                pool.memset(rank[:, :, e:e + 1], float(E - e)).then_inc(const_base, 1)
                pool.memset(slot0[:, :, e:e + 1], float(C * e)).then_inc(const_base, 1)
            pool.iota(token[:, :], [[P, NQ]], base=0, channel_multiplier=1,
                      allow_small_or_imprecise_dtypes=True).then_inc(const_ready, 1)

            def set_up():
                frame(pool, qk[1], qk_ones[1])
                pool.memset(v_aug[:, :, :, :, :], 0.0).then_inc(v_zero, 1)
                pool.wait_ge(v_zero, 1)
                for sub in range(2):
                    for par in range(2):
                        v = v_aug[:, par, :, :, :].rearrange("p j (n s) w -> p (j n) s w", s=2)[
                            :, :, sub, HW * sub + DH:HW * sub + DH + 1]
                        pool.memset(v, 1.0).then_inc(v_ones, 1)

                pool.memset(ctx_sum[:, :, :], 0.0).then_inc(const_base, 1)
                pool.memset(ctx_all[:, FULL, :], 0.0).then_inc(const_base, 1)
                pool.wait_ge(const_base, 5 + 2 * E + 2)
                pool.wait_ge(dead_found, 2)
                found = pool.value_load(any_dead[0:1, 0:1])
                with pool.If(found):
                    with pool.Fori(0, B) as i:
                        pool.dma_start(ctx_all[:, 0:FULL, :], ctx[bass.ds(i, 1), 0:FULL * P, :]
                                       .rearrange("o (p c) d -> p (o c) d", c=FULL)).then_inc(all_in, 16)
                        pool.dma_start(ctx_all[0:REST, FULL, :], ctx[bass.ds(i, 1), FULL * P:LK, :]
                                       .rearrange("o p d -> p (o d)")).then_inc(all_in, 16)
                        wait_apart(pool, all_in, i * 32 + 32, pool_passed)
                        for n in range(FULL + 1):
                            one = ctx_sum[:, bass.ds(i, 1), :]
                            pool.tensor_tensor(one, one, ctx_all[:, n:n + 1, :], ALU.add).then_inc(all_add, 1)
                            wait_apart(pool, all_add, i * (FULL + 1) + (n + 1), pool_passed)
                pool.memset(mark[:, :], 0.0).then_inc(csum_ready, 1)

            def tick(batches, on):
                p, a, b, c, d, e, f = batches
                in_p, in_a, in_b, in_c, in_d, in_e, in_f = on

                def mask_far(quad):
                    if in_c:
                        wait_apart(pool, t_exp, c.count(LOADS, 3 * quad + 2), pool_passed)
                        v = pt[:, quad % 2, 0:4 * L].rearrange("p (h q) -> p h q", q=L)[:, :, 0:P]
                        pool.affine_select(out=v, in_=v, compare_op=ALU.is_ge, fill=0.0, base=0,
                                           pattern=[[0, 4], [1, P]], channel_multiplier=-1).then_inc(t_masked, 1)

                def mask_near(quad):
                    if in_c:
                        wait_apart(pool, t_exp, c.count(LOADS, 3 * quad + 3), pool_passed)
                        v = pt[:, quad % 2, 4 * L:4 * (L + P)].rearrange("p (h q) -> p h q", q=P)
                        pool.affine_select(out=v, in_=v, compare_op=ALU.is_ge, fill=0.0, base=0,
                                           pattern=[[0, 4], [1, P]], channel_multiplier=-1).then_inc(t_masked, 1)

                def dispatch(j):
                    if in_f:
                        if j == 0:
                            wait_apart(pool, gated, f.count(2, 2), pool_passed)
                            wait_apart(pool, rs, f.count(8, 8), pool_passed)
                        pool.indirect_dma_start(
                            out=rows_dram, out_offset=bass.IndirectOffsetOnAxis(ap=slot_i[:, f.par, j:j + 1], axis=0),
                            in_=rows[:, f.par, j, :], in_offset=None, bounds_check=N - 1, oob_is_err=False,
                        ).then_inc(sent[f.par], 16)

                if in_e:
                    pool.wait_ge(lnb, e.count(6, 5))
                    pool.tensor_tensor(lnb_rs[:, :], lnb_ve[:, :], half[:, :], ALU.pow).then_inc(lnb_pow, 1)
                mask_far(0)
                mask_near(0)
                dispatch(0)
                mask_far(1)
                mask_near(1)
                if in_p:
                    pool.wait_ge(lna, p.count(6, 5))
                    pool.tensor_tensor(lna_rs[:, :], lna_ve[:, :], half[:, :], ALU.pow).then_inc(lna_pow, 1)
                dispatch(1)
                mask_far(2)
                mask_near(2)
                mask_far(3)
                mask_near(3)
                if in_e and isinstance(e.i, int) and e.k == 0:
                    pool.wait_ge(fill_out, 16 * FILLS)

            ticks(pool, tick, after_first=set_up)

            for par in range(2):
                pool.wait_ge(x2_out[par], Batch(0, B - 2 + par).landed(1))
                pool.wait_ge(sent[par], Batch(0, B - 2 + par).landed(NQ))

            def expert(e):
                wait_apart(pool, eo, e.count(2 + CC, 2 + CC), pool_passed)
                for j in range(CC):
                    pool.indirect_dma_start(
                        out=out_rows, out_offset=bass.IndirectOffsetOnAxis(ap=e_tok[:, e.par, j:j + 1], axis=0),
                        in_=e_out[:, e.par, j, :], in_offset=None, bounds_check=N - 1, oob_is_err=False,
                    ).then_inc(eo_out[e.par], 16)

            experts(pool, expert)
            for par in range(2):
                pool.wait_ge(eo_out[par], Batch(0, E - 2 + par).landed(CC))

        @block.scalar
        def _(act):
            act.wait_ge(g_in, 32)
            act.activation(tg[:, :], gates[:, :], ACT.Tanh).then_inc(tg_ready, 1)

            def means():
                act.wait_ge(csum_ps, 1)
                act.activation(csum_t[:, :], mb[:, 0:B], ACT.Copy).then_inc(csum_sb, 1)
                act.wait_ge(vmean_ps, 1)
                act.activation(vmean[:, :], mb[0:B, 0:D], ACT.Copy).then_inc(vmean_sb, 1)

            def tick(batches, on):
                p, a, b, c, d, e, f = batches
                in_p, in_a, in_b, in_c, in_d, in_e, in_f = on

                def exp(i):
                    if in_c:
                        quad = i // 3
                        if i % 3 == 0:
                            wait(act, pv, c.count(QUADS, quad - 1))
                        act.wait_ge(t_made, c.count(LOADS, i + 1))
                        act.activation(pt[:, quad % 2, 512 * (i % 3):512 * (i % 3) + 512], t_ps[i % 2][:, :], ACT.Exp,
                                       scale=SCALE).then_inc(t_exp, 1)

                def qk_part(n):
                    if in_a:
                        act.wait_ge(qk_ps, a.count(3, n + 1))
                        if n == 0:
                            wait(act, parts_out[a.par], a.minus(2).landed(5))
                        act.activation(parts[:, a.par, n, :], mb[:, :], ACT.Copy).then_inc(qk_sb, 1)

                def max_rows(bt, hf):
                    act.wait_ge(m_ps, bt.count(2, hf + 1))
                    wait(act, m_in[hf][1 - bt.par], bt.minus(1).landed(1))
                    act.activation(m3_t[:, hf, :], mc_b[0:24, 0:L], ACT.Copy).then_inc(m_sb, 1)

                if in_a:
                    act.wait_ge(xt_ps, a.count(1, 1))
                    wait(act, qk_ps, a.count(3, 0))
                    act.activation(xn_t[:, :], ma[:, 0:L], ACT.Copy).then_inc(xt_sb, 1)
                exp(0)
                qk_part(0)
                exp(1)
                qk_part(1)
                if in_d:
                    act.wait_ge(pv, d.count(QUADS, QUADS))
                    wait(act, o_turned, d.count(1, 0))
                    act.activation(o_sb[:, :], o_ps[:, :], ACT.Copy).then_inc(o_copied, 1)
                exp(2)
                if in_b:
                    act.wait_ge(v_ps, b.count(1, 1))
                    wait(act, pv, b.minus(2).count(QUADS, QUADS))
                    if isinstance(b.i, int) and b.k == 0:
                        act.wait_ge(v_ones, 4)
                    for j in range(NQ):
                        for sub in range(2):
                            dst = v_aug[:, b.par, j, :, :].rearrange("p (n s) w -> p n s w", s=2)[:, :, sub,
                                                                                                HW * sub:HW * sub + DH]
                            src = ma[:, j * D:(j + 1) * D].rearrange("p (n s d) -> p n s d", s=2, d=DH)[:, :, sub, :]
                            act.activation(dst, src, ACT.Copy).then_inc(v_sb, 1)
                if in_c:
                    max_rows(c, 1)
                exp(3)
                if in_e:
                    act.wait_ge(lnb, e.count(6, 6))
                    wait(act, x2t_ps, e.count(1, 0))
                    wait(act, gated, e.count(2, 0))
                    for j in range(NQ):
                        act.activation(x2n[:, j, :], rows[:, e.par, j, D:2 * D], ACT.Identity, bias=lnb_nb[:, j:j + 1],
                                       scale=lnb_rs[:, j:j + 1]).then_inc(x2n_ready, 1)
                exp(4)
                qk_part(2)
                if in_e:
                    act.wait_ge(x2t_ps, e.count(1, 1))
                    wait(act, lg_ps, e.count(1, 0))
                    act.activation(x2n_t[:, :], ma[:, 0:L], ACT.Copy).then_inc(x2t_sb, 1)
                exp(5)
                exp(6)
                exp(7)
                exp(8)
                if in_d:
                    act.wait_ge(cx_ps, d.count(1, 1))
                    wait(act, at_ps, d.count(1, 0))
                    act.activation(cx_t[:, :], ma[:, 0:L], ACT.Copy).then_inc(cx_sb, 1)
                if in_e:
                    act.wait_ge(rt, e.count(6, 3))
                    act.activation(lg_e[:, :, :], lg_d[:, :, :], ACT.Exp).then_inc(e_ready, 1)
                if in_b:
                    max_rows(b, 0)
                exp(9)
                if in_p:
                    act.wait_ge(lna, p.count(6, 6))
                    wait(act, xt_ps, p.count(1, 0))
                    for j in range(NQ):
                        act.activation(xn[:, j, :], x_in[:, p.par, j, :], ACT.Identity, bias=lna_nb[:, j:j + 1],
                                       scale=lna_rs[:, j:j + 1]).then_inc(xn_ready, 1)
                exp(10)
                if in_e:
                    act.wait_ge(gs, e.count(5, 2))
                    wait(act, sent[e.par], e.minus(2).landed(NQ))
                    for j in range(NQ):
                        act.activation(rows[:, e.par, j, 0:D], x2n[:, j, :], ACT.Identity, bias=zero[:, :],
                                       scale=gate[:, j:j + 1]).then_inc(gated, 1)
                exp(11)

            ticks(act, tick, means)

            def hidden(e):
                act.wait_ge(eh_ps, e.count(1, 1))
                wait(act, eo_ps, e.minus(1).count(1, 0))
                act.wait_ge(e1_in[e.par], e.landed(2))
                act.activation(e_h[:, e.par, :], eh_bank[e.par][:, :], ACT.Relu, bias=b1_s[:, e.par, :]
                               ).then_inc(eh_sb, 1)

            def expert(e):
                if not (isinstance(e.i, int) and e.k == 0):
                    hidden(e.minus(1))
                act.wait_ge(ei_ps, e.count(1, 1))
                wait(act, eh_ps, e.minus(1).count(1, 0))
                act.activation(e_in_t[:, e.par, :], ei_bank[e.par][:, :], ACT.Copy).then_inc(ei_sb, 1)

            experts(act, expert)
            hidden(Batch(0, E - 1))

        @block.vector
        def _(dve):
            dve.memset(half[:, :], -0.5).then_inc(vconst, 1)
            dve.memset(zero[:, :], 0.0).then_inc(vconst, 1)
            dve.memset(ones_b[:, :], 1.0).then_inc(vconst, 1)
            dve.memset(mean_w[:, :], 1.0 / LK).then_inc(vconst, 1)
            dve.memset(carry[:, :, :], 0.0).then_inc(vconst, 1)

            dve.memset(filler[:, :], FAR).then_inc(fill_set, 1)
            dve.wait_ge(mask_in, 16)
            dve.tensor_scalar(kb_s[:, :], mask_s[:, :], 0, NEG, ALU.is_equal, ALU.mult).then_inc(kb_ready, 1)
            dve.wait_ge(mask0_in, 16)
            dve.tensor_scalar(no_key[:, :], mask0[:, :], 0, None, ALU.is_equal).then_inc(dead_found, 1)
            dve.wait_ge(dead_found, 1)
            dve.tensor_reduce(any_dead[:, :], no_key[:, :], AX_X, ALU.max).then_inc(dead_found, 1)

            def tick(batches, on):
                p, a, b, c, d, e, f = batches
                in_p, in_a, in_b, in_c, in_d, in_e, in_f = on

                def reduce_max(i):
                    if in_b:
                        dve.wait_ge(s_made, b.count(LOADS, i + 1))
                        hs = heads(i // 3)
                        v = s_ps[i % 2][:, :]
                        if i % 3 < 2:
                            lo = hs[2 * (i % 3)]
                            o, v = max_far[:, lo:lo + 3:2, :], v.rearrange("p (h s k) -> p h s k", s=2, k=P)
                        else:
                            o, v = max_near[:, hs[0]:hs[0] + 7:2], v.rearrange("p (h k) -> p h k", k=P)
                        dve.tensor_reduce(o, v, AX_X, ALU.max).then_inc(s_max, 1)

                class SplitMax:
                    def __init__(self, bt, hf):
                        self.ch, self.bt, self.hf = Steps(dve, mch, bt, 15, 8 * hf), bt, hf
                        self.h8 = slice(8 * hf, 8 * hf + 8)
                        self.m = m3[:, hf, :, :, :]

                    def largest(self):
                        dve.wait_ge(s_max, self.bt.count(LOADS, (self.hf + 1) * LOADS // 2))
                        wait(dve, mch, self.bt.count(15, 8 * self.hf))
                        self.ch.did(dve.tensor_tensor(max_tmp[:, :], max_far[:, self.h8, 0], max_far[:, self.h8, 1],
                                                      ALU.max))

                    def negate(self):
                        self.ch.settle()
                        self.ch.did(dve.tensor_scalar(neg_max[:, 1, :], max_tmp[:, :], MAX_FLOOR, -1.0,
                                                      ALU.max, ALU.mult))
                        self.ch.did(dve.tensor_scalar(neg_max[:, 0, :], max_near[:, self.h8], MAX_FLOOR, -1.0,
                                                      ALU.max, ALU.mult))

                    def hi(self):
                        self.ch.settle()
                        wait(dve, m_ps, self.bt.minus(1).count(2, self.hf + 1))
                        self.ch.did(dve.tensor_copy(self.m[:, :, 0, :], neg_max[:, :, :]))

                    def rest(self):
                        self.ch.settle()
                        self.ch.did(dve.tensor_tensor(neg_res[:, :, :], neg_max[:, :, :], self.m[:, :, 0, :],
                                                      ALU.subtract))

                    def mid(self):
                        self.ch.settle()
                        self.ch.did(dve.tensor_copy(self.m[:, :, 1, :], neg_res[:, :, :]))

                    def lo(self):
                        self.ch.settle()
                        self.ch.did(dve.tensor_tensor(self.m[:, :, 2, :], neg_res[:, :, :], self.m[:, :, 1, :],
                                                      ALU.subtract))

                    def find_dead(self):
                        wait(dve, cxf, self.bt.minus(2).count(2, 2))
                        self.ch.did(dve.tensor_scalar(dead[:, self.bt.par, :, :], neg_max[:, :, 0:1], DEAD_AT, None,
                                                      ALU.is_ge))

                class Norm:
                    def __init__(self, sem, bt, mv, ve, rstd, nb, powd):
                        self.ch, self.bt, self.powd = Steps(dve, sem, bt, 6), bt, powd
                        self.mv, self.ve, self.rstd, self.nb = mv, ve, rstd, nb

                    def stats(self, src, stats):
                        wait(dve, self.ch.sem, self.bt.count(6, 0))
                        for j in range(NQ):
                            self.ch.did(dve.bn_stats(stats[:, j, :], src[:, j, :]))

                    def mean(self, stats):
                        self.ch.n = NQ
                        wait_apart(dve, self.ch.sem, self.bt.count(6, NQ), dve_passed)
                        for j in range(NQ):
                            self.ch.did(dve.bn_aggr(self.mv[:, j, :], stats[:, j, :]))

                    def variance(self, readers):
                        wait(dve, readers, self.bt.count(2, 0))
                        self.ch.settle()
                        self.ch.did(dve.tensor_scalar(self.ve[:, :], self.mv[:, :, 1], EPS, None, ALU.add))

                    def offset(self):
                        dve.wait_ge(self.powd, self.bt.count(1, 1))
                        self.ch.did(dve.scalar_tensor_tensor(out=self.nb[:, :], in0=self.mv[:, :, 0], scalar=-1.0,
                                                             in1=self.rstd[:, :], op0=ALU.mult, op1=ALU.mult))

                if in_b:
                    max_0 = SplitMax(b, 0)
                if in_c:
                    max_1 = SplitMax(c, 1)
                norm_p = Norm(lna, p, lna_mv, lna_ve, lna_rs, lna_nb, lna_pow)
                norm_d = Norm(lnb, d, lnb_mv, lnb_ve, lnb_rs, lnb_nb, lnb_pow)
                norm_e = Norm(lnb, e, lnb_mv, lnb_ve, lnb_rs, lnb_nb, lnb_pow)
                cx = Steps(dve, cxn, d, 3)
                lg_steps = Steps(dve, rt, e, 6)
                gate_steps = Steps(dve, gs, e, 5)
                place = Steps(dve, rs, f, 8, 2)
                o_view = ma[:, :].rearrange("p (j h w) -> p j h w", j=NQ, w=HW)

                def o_sums():
                    dve.wait_ge(o_turned, d.count(1, 1))
                    cx.did(dve.tensor_tensor(l_sum[:, :, :], o_view[:, :, :, DH],
                                             dead[:, d.par, :, :].to_broadcast([P, NQ, H]), ALU.add))

                def o_inverse():
                    cx.settle()
                    cx.did(dve.reciprocal(l_inv[:, :, :], l_sum[:, :, :]))

                def o_scaled():
                    cx.settle()
                    wait(dve, cxf, d.count(2, 0))
                    cx.did(dve.tensor_tensor(cx_n[:, :, :, :], o_view[:, :, :, 0:DH],
                                             l_inv[:, :, :].unsqueeze(3).to_broadcast([P, NQ, H, DH]), ALU.mult))

                def o_fixed():
                    cx.settle()
                    dve.wait_ge(res_got[d.par], d.landed(2))
                    wait(dve, cx_ps, d.count(1, 0))
                    for j in range(NQ):
                        dve.scalar_tensor_tensor(
                            out=cx_f[:, j, :], in0=vm_in[:, d.par, :], scalar=dead[:, d.par, j, :],
                            in1=cx_n[:, j, :, :].rearrange("p h d -> p (h d)"), op0=ALU.mult, op1=ALU.add
                        ).then_inc(cxf, 1)

                def residual():
                    dve.wait_ge(at_ps, d.count(1, 1))
                    dve.wait_ge(res_got[d.par], d.landed(2))
                    if isinstance(d.i, int) and d.k == 0:
                        dve.wait_ge(tg_ready, 1)
                    wait(dve, sent[d.par], d.minus(2).landed(NQ))
                    wait(dve, x2_out[d.par], d.minus(2).landed(1))
                    dve.scalar_tensor_tensor(out=rows[:, d.par, :, D:2 * D],
                                             in0=ma[:, 0:L].rearrange("p (j d) -> p j d", d=D),
                                             scalar=tg[:, 0:1], in1=x_res[:, d.par, :, :], op0=ALU.mult,
                                             op1=ALU.add).then_inc(x2_ready, 1)

                def logits():
                    dve.wait_ge(lg_ps, e.count(1, 1))
                    if isinstance(e.i, int) and e.k == 0:
                        dve.wait_ge(w_in, 96)
                        dve.wait_ge(const_base, 5 + 2 * E)
                    wait(dve, rt, e.count(6, 0))
                    lg_steps.did(dve.tensor_tensor(lg[:, :, :], mb[:, 0:NQ * E].rearrange("p (j e) -> p j e", e=E),
                                                   br_s[:, :].unsqueeze(1).to_broadcast([P, NQ, E]), ALU.add))

                def logits_max():
                    lg_steps.settle()
                    lg_steps.did(dve.tensor_reduce(lg_max[:, :], lg[:, :, :], AX_X, ALU.max))

                def logits_less():
                    lg_steps.settle()
                    wait(dve, e_ready, e.count(1, 0))
                    lg_steps.did(dve.tensor_tensor(lg_d[:, :, :], lg[:, :, :],
                                                   lg_max[:, :].unsqueeze(2).to_broadcast([P, NQ, E]), ALU.subtract))

                def ranks():
                    lg_steps.settle()
                    lg_steps.did(dve.scalar_tensor_tensor(out=w_rank[:, :, :], in0=lg_d[:, :, :], scalar=0.0,
                                                          in1=rank[:, :, :].to_broadcast([P, NQ, E]),
                                                          op0=ALU.is_ge, op1=ALU.mult))

                def best_rank():
                    lg_steps.settle()
                    lg_steps.did(dve.tensor_reduce(w_best[:, :], w_rank[:, :, :], AX_X, ALU.max))

                def chosen():
                    lg_steps.settle()
                    wait(dve, cum_ps, e.count(1, 0))
                    wait(dve, rs, e.count(8, 0))
                    lg_steps.did(dve.tensor_tensor(onehot[:, :, :], w_rank[:, :, :],
                                                   w_best[:, :].unsqueeze(2).to_broadcast([P, NQ, E]), ALU.is_equal))

                def gates_sum():
                    dve.wait_ge(e_ready, e.count(1, 1))
                    wait(dve, gs, e.count(5, 0))
                    gate_steps.did(dve.tensor_reduce(e_sum[:, :], lg_e[:, :, :], AX_X, ALU.add))

                def gates_made():
                    gate_steps.settle()
                    wait(dve, gated, e.count(2, 0))
                    gate_steps.did(dve.reciprocal(gate[:, :], e_sum[:, :]))

                def row_ends():
                    gate_steps.settle()
                    wait(dve, sent[e.par], e.minus(2).landed(NQ))
                    ro = rows[:, e.par, :, :]
                    gate_steps.did(dve.tensor_scalar(ro[:, :, 2 * D], gate[:, :], tg[:, 1:2], None, ALU.mult))
                    if isinstance(e.i, int) and e.k == 0:
                        dve.wait_ge(const_ready, 6)
                    gate_steps.did(dve.tensor_copy(ro[:, :, 2 * D + 1], token[:, :]))

                def next_tokens():
                    gate_steps.settle()
                    gate_steps.did(dve.tensor_scalar(token[:, :], token[:, :], float(L), None, ALU.add))

                def queue_places():
                    dve.wait_ge(cum_ps, e.count(1, 1))
                    wait(dve, rs, e.count(8, 0))
                    n = NQ * E
                    dve.tensor_tensor(pos[:, :, :], mc[:, 0:n].rearrange("p (j e) -> p j e", e=E),
                                      carry[:, :, :].to_broadcast([P, NQ, E]), ALU.add).then_inc(rs, 1)

                def queue_lengths():
                    dve.wait_ge(rs, e.count(8, 1))
                    n = NQ * E
                    dve.tensor_tensor(carry[:, 0, :], carry[:, 0, :], mc[:, n:n + E], ALU.add).then_inc(rs, 1)

                def pick():
                    place.settle()
                    place.did(dve.tensor_tensor(picked[:, 0:NQ, :], pos[:, :, :], onehot[:, :, :], ALU.mult))
                    place.did(dve.tensor_tensor(picked[:, NQ:2 * NQ, :], onehot[:, :, :],
                                                slot0[:, :, :].to_broadcast([P, NQ, E]), ALU.mult))

                def pick_sums():
                    place.settle()
                    place.did(dve.tensor_reduce(pick_sum[:, :], picked[:, :, :], AX_X, ALU.add))

                def slots():
                    place.settle()
                    place.did(dve.tensor_tensor(slot[:, :], pick_sum[:, 0:NQ], pick_sum[:, NQ:2 * NQ], ALU.add))
                    place.did(dve.tensor_scalar(over[:, :], pick_sum[:, 0:NQ], float(C), FAR, ALU.is_ge, ALU.mult))

                def slots_whole():
                    place.settle()
                    place.did(dve.tensor_tensor(slot_i[:, f.par, :], slot[:, :], over[:, :], ALU.add))

                if in_c:
                    max_1.largest()
                if in_e:
                    norm_e.mean(lnb_st)
                if in_c:
                    max_1.negate()
                reduce_max(0)
                if in_c:
                    max_1.hi()
                if in_e:
                    norm_e.variance(x2n_ready)
                if in_c:
                    max_1.rest()
                if in_f:
                    pick()
                reduce_max(1)
                if in_c:
                    max_1.mid()
                if in_f:
                    pick_sums()
                if in_c:
                    max_1.lo()
                reduce_max(2)
                if in_f:
                    slots()
                if in_e:
                    norm_e.offset()
                if in_f:
                    slots_whole()
                reduce_max(3)
                if in_p:
                    dve.wait_ge(x_got[p.par], p.landed(1))
                    norm_p.stats(x_in[:, p.par, :, :], lna_st)
                reduce_max(4)
                if in_p:
                    norm_p.mean(lna_st)
                reduce_max(5)
                if in_p:
                    norm_p.variance(xn_ready)
                if in_b:
                    max_0.largest()
                if in_d:
                    o_sums()
                if in_b:
                    max_0.negate()
                if in_d:
                    o_inverse()
                reduce_max(6)
                if in_b:
                    max_0.hi()
                if in_d:
                    o_scaled()
                if in_b:
                    max_0.rest()
                if in_e:
                    logits()
                if in_d:
                    o_fixed()
                reduce_max(7)
                if in_b:
                    max_0.mid()
                if in_e:
                    logits_max()
                if in_b:
                    max_0.lo()
                if in_e:
                    logits_less()
                reduce_max(8)
                if in_e:
                    ranks()
                if in_b:
                    max_0.find_dead()
                if in_e:
                    best_rank()
                if in_p:
                    norm_p.offset()
                if in_e:
                    chosen()
                reduce_max(9)
                if in_e:
                    gates_sum()
                reduce_max(10)
                if in_e:
                    gates_made()
                if in_d:
                    residual()
                if in_e:
                    row_ends()
                reduce_max(11)
                if in_e:
                    queue_places()
                if in_d:
                    dve.wait_ge(x2_ready, d.count(1, 1))
                    norm_d.stats(rows[:, d.par, :, D:2 * D], lnb_st)
                if in_e:
                    next_tokens()
                    queue_lengths()

            ticks(dve, tick, after_first=lambda: frame(dve, qk[0], qk_ones[0]))

            def expert(e):
                ch = Steps(dve, eo, e, 2 + CC)
                wait(dve, eo, e.count(2 + CC, 0))
                dve.wait_ge(eo_ps, e.count(1, 1))
                dve.wait_ge(e2_in[e.par], e.landed(2))
                dve.wait_ge(er_in[e.par], e.landed(1))
                if not (isinstance(e.i, int) and e.k < 2):
                    dve.wait_ge(eo_out[e.par], e.minus(2).landed(CC))
                ch.did(dve.tensor_tensor(e_tmp[:, :, :], eo_bank[e.par][:, :].rearrange("p (c d) -> p c d", d=D),
                                         b2_s[:, e.par, :].unsqueeze(1).to_broadcast([P, CC, D]), ALU.add))
                ch.did(dve.tensor_copy(e_tok[:, e.par, :], e_rest[:, e.par, :, D + 1]))
                ch.settle()
                for j in range(CC):
                    ch.did(dve.scalar_tensor_tensor(out=e_out[:, e.par, j, :], in0=e_tmp[:, j, :],
                                                    scalar=e_rest[:, e.par, j, D:D + 1],
                                                    in1=e_rest[:, e.par, j, 0:D], op0=ALU.mult, op1=ALU.add))

            experts(dve, expert)

        @block.tensor
        def _(pe):
            def means():
                pe.wait_ge(qk_sb, 3)
                pe.wait_ge(csum_ready, 1)
                pe.wait_ge(vconst, 5)
                for n in range(B):
                    last = pe.matmul(mb[:, n:n + 1], ctx_sum[:, n, :], mean_w[:, :], start=True, stop=True)
                last.then_inc(csum_ps, 1)
                pe.wait_ge(csum_sb, 1)
                pe.matmul(mb[0:B, 0:D], csum_t[:, :], wv_s[:, :], start=True, stop=True).then_inc(vmean_ps, 1)

            def tick(batches, on):
                p, a, b, c, d, e, f = batches
                in_p, in_a, in_b, in_c, in_d, in_e, in_f = on

                def s_load(i):
                    if not in_b:
                        return
                    q = qk[b.par]
                    if i % (LOADS // 2) == 0:
                        pe.wait_ge(stack_in[i // (LOADS // 2)][b.par], b.landed(2))
                    wait(pe, s_max, b.count(LOADS, i - 1))
                    hs, bank = heads(i // 3), s_ps[i % 2]
                    if i % 3 < 2:
                        for n, h in enumerate(hs[2 * (i % 3):2 * (i % 3) + 2]):
                            pe.matmul(bank[:, L * n:L * n + L], q[0:SROWS, h, P:L], q[0:SROWS, h, L:2 * L],
                                      start=n == 0, stop=False, skip_group_check=True)
                        o = bank[:, :].rearrange("p (h s k) -> p h s k", s=2, k=P)[:, :, 1, :]
                        m = 2
                    else:
                        for n, h in enumerate(hs):
                            pe.matmul(bank[:, P * n:P * n + P], q[0:SROWS, h, 0:P], q[0:SROWS, h, L:L + P],
                                      start=n == 0, stop=False, skip_group_check=True)
                        o = bank[:, :].rearrange("p (h k) -> p h k", k=P)
                        m = 4
                    pe.matmul(o, ident_b[:, :], causal[:, :].unsqueeze(1).to_broadcast([P, m, P]), start=False,
                              stop=True, skip_group_check=True).then_inc(s_made, 1)

                def t_load(i):
                    if not in_c:
                        return
                    q = qk[c.par]
                    if i % (LOADS // 2) == 0:
                        pe.wait_ge(m_in[i // (LOADS // 2)][c.par], c.landed(1))
                    wait(pe, t_exp, c.count(LOADS, i - 1))
                    hs, bank = heads(i // 3), t_ps[i % 2]
                    if i % 3 < 2:
                        for n, h in enumerate(hs[2 * (i % 3):2 * (i % 3) + 2]):
                            last = pe.matmul(bank[:, L * n:L * n + L], q[0:TROWS, h, L:L + P], q[0:TROWS, h, 0:L],
                                             start=True, stop=True)
                    else:
                        for n, h in enumerate(hs):
                            last = pe.matmul(bank[:, P * n:P * n + P], q[0:TROWS, h, L + P:2 * L],
                                             q[0:TROWS, h, P:L], start=True, stop=True)
                    last.then_inc(t_made, 1)

                def values(bt, quad):
                    pe.wait_ge(t_exp, bt.count(LOADS, 3 * quad + 3))
                    pe.wait_ge(t_masked, bt.count(2 * QUADS, 2 * quad + 2))
                    if quad == 0:
                        pe.wait_ge(v_sb, bt.count(4, 4))
                        wait(pe, o_copied, bt.count(1, 0))
                    hf = quad // 2
                    for g, h in enumerate(heads(quad)):
                        pe.matmul(o_ps[32 * g:32 * g + 32, hf * L:hf * L + L], v_aug[:, bt.par, 0, h, :],
                                  pt[:, quad % 2, L * g:L * g + L], start=quad == 0, stop=False,
                                  skip_group_check=True)
                    for g, h in enumerate(heads(quad)):
                        last = pe.matmul(o_ps[32 * g:32 * g + 32, hf * L + P:hf * L + L], v_aug[:, bt.par, 1, h, :],
                                         pt[:, quad % 2, 4 * L + P * g:4 * L + P * g + P], start=False,
                                         stop=quad == QUADS - 1, skip_group_check=True)
                    last.then_inc(pv, 1)

                def turn_max(bt, hf):
                    pe.wait_ge(mch, bt.count(15, 7 + 8 * hf))
                    wait(pe, m_sb, bt.count(2, hf))
                    for j in range(NQ):
                        last = pe.transpose(mc_b[0:24, j * P:j * P + P],
                                            m3[:, hf, j, :, :].rearrange("p a h -> p (a h)"), ident_b[:, :])
                    last.then_inc(m_ps, 1)

                def less_part(n):
                    if in_a:
                        pe.wait_ge(qk_sb, a.count(3, n + 1))
                        pe.matmul(mb[:, :], minus_b[:, :], parts[:, a.par, n, :], start=False, stop=n == 1,
                                  skip_group_check=True).then_inc(qk_ps, 1)

                s_load(0)
                t_load(0)
                if in_a:
                    wait(pe, rt, e.count(6, 0))
                    wait(pe, qk_sb, a.count(3, 0))
                    if isinstance(a.i, int) and a.k == 0:
                        pe.wait_ge(w_in, 96)
                    if isinstance(a.i, int) and a.k == 1:
                        pe.wait_ge(vmean_sb, 1)
                    pe.wait_ge(ctx_got[a.par], a.landed(1))
                    pe.matmul(mb[:, L:2 * L], wk_s[:, :], ctx_in[:, a.par, :], start=True, stop=False,
                              skip_group_check=True)
                    pe.wait_ge(xt_sb, a.count(1, 1))
                    pe.matmul(mb[:, 0:L], wq_s[:, :], xn_t[:, :], start=False, stop=False,
                              skip_group_check=True).then_inc(qk_ps, 1)
                s_load(1)
                t_load(1)
                less_part(0)
                if in_d:
                    values(d, QUADS - 1)
                if in_b:
                    if in_a:
                        pe.wait_ge(xt_sb, a.count(1, 1))
                    wait(pe, x2_ready, e.count(1, 1))
                    for j in range(NQ):
                        last = pe.matmul(ma[:, j * D:(j + 1) * D], ctx_in[:, b.par, j * P:(j + 1) * P], wv_s[:, :],
                                         start=True, stop=True)
                    last.then_inc(v_ps, 1)
                s_load(2)
                t_load(2)
                if in_c:
                    wait(pe, rs, f.count(8, 2))
                    turn_max(c, 1)
                s_load(3)
                t_load(3)
                s_load(4)
                less_part(1)
                t_load(4)
                if in_c:
                    values(c, 0)
                if in_e:
                    pe.wait_ge(x2n_ready, e.count(2, 2))
                    if in_b:
                        pe.wait_ge(v_sb, b.count(4, 4))
                    if in_a:
                        pe.wait_ge(xt_sb, a.count(1, 1))
                    for j in range(NQ):
                        last = pe.transpose(ma[:, j * P:j * P + P], x2n[:, j, :], ident[:, :])
                    last.then_inc(x2t_ps, 1)
                s_load(5)
                t_load(5)
                if in_d:
                    if in_e:
                        pe.wait_ge(x2t_sb, e.count(1, 1))
                    if in_b:
                        pe.wait_ge(v_sb, b.count(4, 4))
                    pe.wait_ge(o_copied, d.count(1, 1))
                    for j in range(NQ):
                        for hf in range(2):
                            n = j * 2 + hf
                            last = pe.transpose(ma[:, n * P:n * P + P], o_sb[:, hf * L + j * P:hf * L + j * P + P],
                                                ident[:, :])
                    last.then_inc(o_turned, 1)
                if in_e:
                    pe.wait_ge(x2t_sb, e.count(1, 1))
                    if in_a:
                        pe.wait_ge(qk_sb, a.count(3, 3))
                    wait(pe, rt, e.count(6, 0))
                    for j in range(NQ):
                        last = pe.matmul(mb[:, E * j:E * j + E], x2n_t[:, j * P:(j + 1) * P], wr_s[:, :],
                                         start=True, stop=True)
                    last.then_inc(lg_ps, 1)
                s_load(6)
                t_load(6)
                s_load(7)
                t_load(7)
                if in_c:
                    values(c, 1)
                s_load(8)
                t_load(8)
                if in_b:
                    if in_c:
                        pe.wait_ge(m_sb, c.count(2, 2))
                    turn_max(b, 0)
                s_load(9)
                if in_d:
                    pe.wait_ge(cxf, d.count(2, 2))
                    for j in range(NQ):
                        last = pe.transpose(ma[:, j * P:j * P + P], cx_f[:, j, :], ident[:, :])
                    last.then_inc(cx_ps, 1)
                t_load(9)
                s_load(10)
                t_load(10)
                if in_d:
                    pe.wait_ge(cx_sb, d.count(1, 1))
                    for j in range(NQ):
                        last = pe.matmul(ma[:, j * D:(j + 1) * D], cx_t[:, j * P:(j + 1) * P], wo_s[:, :],
                                         start=True, stop=True)
                    last.then_inc(at_ps, 1)
                if in_c:
                    values(c, 2)
                if in_e:
                    pe.wait_ge(rt, e.count(6, 6))
                    if in_b:
                        pe.wait_ge(m_sb, b.count(2, 1))
                    elif in_c:
                        pe.wait_ge(m_sb, c.count(2, 2))
                    wait(pe, rs, f.count(8, 2))
                    n = NQ * E
                    for j in range(NQ + 1):
                        o = mc[:, E * j:E * j + E]
                        for jj in range(min(j + 1, NQ)):
                            last = pe.matmul(o, (tri if jj == j else ones_b)[:, :], onehot[:, jj, :],
                                             start=jj == 0, stop=jj == min(j, NQ - 1))
                    last.then_inc(cum_ps, 1)
                s_load(11)
                t_load(11)
                if in_p:
                    if isinstance(p.i, int) and p.k == 0:
                        pe.wait_ge(const_ready, 5)
                    pe.wait_ge(xn_ready, p.count(2, 2))
                    wait(pe, x2_ready, d.count(1, 1))
                    wait(pe, v_sb, b.count(4, 4))
                    wait(pe, xt_sb, p.count(1, 0))
                    for j in range(NQ):
                        last = pe.transpose(ma[:, j * P:j * P + P], xn[:, j, :], ident[:, :])
                    last.then_inc(xt_ps, 1)

            ticks(pe, tick, means)

            pe.wait_ge(s_max, LOADS * B)
            pe.wait_ge(t_exp, LOADS * B)
            pe.wait_ge(x2_ready, B)
            pe.wait_ge(x2t_sb, B)
            pe.wait_ge(rt, 6 * B)

            def second(e):
                pe.wait_ge(e2_in[e.par], e.landed(2))
                pe.wait_ge(eh_sb, e.count(1, 1))
                wait(pe, eo, e.minus(1).count(2 + CC, 1))
                for j in range(CC):
                    last = pe.matmul(eo_bank[e.par][:, j * D:(j + 1) * D], e_h[:, e.par, j * P:(j + 1) * P],
                                     w2_s[:, e.par, :], start=True, stop=True)
                last.then_inc(eo_ps, 1)

            def expert(e):
                pe.wait_ge(ex_in[e.par], e.landed(1))
                wait(pe, ei_sb, e.minus(1).count(1, 0))
                for j in range(CC):
                    last = pe.transpose(ei_bank[e.par][:, j * P:j * P + P], e_in[:, e.par, j, :], ident[:, :])
                last.then_inc(ei_ps, 1)
                if not (isinstance(e.i, int) and e.k == 0):
                    second(e.minus(1))
                pe.wait_ge(ei_sb, e.count(1, 1))
                pe.wait_ge(e1_in[e.par], e.landed(2))
                pe.matmul(eh_bank[e.par][:, :], w1_s[:, e.par, :], e_in_t[:, e.par, :], start=True, stop=True
                          ).then_inc(eh_ps, 1)

            experts(pe, expert)
            second(Batch(0, E - 1))


def kernel(x, ctx_1024, mask_BxS2_if1, g_xattn, g_ffn, L0_xattn_Wq, L0_xattn_Wk, L0_xattn_Wv, L0_xattn_Wo,
           L0_ffn_Wr, L0_ffn_br, L0_ffn_W1, L0_ffn_b1, L0_ffn_W2, L0_ffn_b2):
    import numpy as np
    import concourse.bacc as bacc
    from concourse.bass_utils import run_bass_kernel_spmd

    seen = x.shape[1]
    ctx = np.asarray(ctx_1024)
    b1 = np.asarray(L0_ffn_b1)
    laid = {
        "x": x, "ctx": ctx, "ctx_t": ctx[:, :seen, :].transpose(0, 2, 1), "mask": mask_BxS2_if1,
        "g_xattn": g_xattn, "g_ffn": g_ffn,
        "wq_t": np.asarray(L0_xattn_Wq).T, "wk_t": np.asarray(L0_xattn_Wk).T,
        "wv_t": np.asarray(L0_xattn_Wv).T, "wo_t": np.asarray(L0_xattn_Wo).T,
        "wr": L0_ffn_Wr, "br": L0_ffn_br, "w1": L0_ffn_W1, "b1": b1.reshape(*b1.shape, 1),
        "w2": L0_ffn_W2, "b2": L0_ffn_b2,
    }
    nc = bacc.Bacc("TRN2", target_bir_lowering=False, num_devices=1)
    arrays, args = {}, []
    for name, a in laid.items():
        a = np.ascontiguousarray(a)
        arrays[f"in_{name}"] = a
        args.append(nc.dram_tensor(f"in_{name}", a.shape, mybir.dt.from_np(a.dtype), kind="ExternalInput").ap())
    out = nc.dram_tensor("out_0", x.shape, F32, kind="ExternalOutput").ap()
    build(nc, *args, out)
    r = run_bass_kernel_spmd(nc, [arrays], core_ids=[0])
    return r.results[0]["out_0"]
```
